# Optimizing a Trainium2 kernel written in Bass

```python
import numpy as np
import jax
import jax.numpy as jnp

def _softmax(x, axis=-1):
    return jax.nn.softmax(x, axis=axis)

def _gelu(x):
    return jax.nn.gelu(x, approximate=True)

def _silu(x):
    return jax.nn.silu(x)

def _sigmoid(x):
    return jax.nn.sigmoid(x)

def _layernorm(x, axis=-1, eps=1e-05):
    m = jnp.mean(x, axis=axis, keepdims=True)
    v = jnp.var(x, axis=axis, keepdims=True)
    return (x - m) / jnp.sqrt(v + eps)

def _scatter_add(tgt, idx, src, axis=0):
    return tgt.at[idx].add(src)

def _segment_sum(src, seg, n):
    return jax.ops.segment_sum(src, seg, n)
kernel_name = 'mk_adaln_ffn_d1_seqx_r4_ede8f9'

def setup_inputs(seed: int=0):
    np.random.seed(seed)
    _w = jnp.asarray

    def _rec_inputs():
        import jax
        import jax.numpy as jnp
        _rk = jax.random.key(seed)
        x = -0.000125 + 0.9999 * jax.random.normal(jax.random.fold_in(_rk, 1), (32, 256, 256), jnp.float32)
        _lenS = 256 - jax.random.randint(jax.random.fold_in(_rk, 7), (32,), 0, max(1, 256 // 4) + 1, jnp.int32)
        _lenS2 = 256 - jax.random.randint(jax.random.fold_in(_rk, 8), (32,), 0, max(1, 256 // 4) + 1, jnp.int32)
        cond_1024 = 0.00513981 + 1.0024 * jax.random.normal(jax.random.fold_in(_rk, 11), (32, 256), jnp.float32)
        return (x, cond_1024)
    x, cond_1024 = _rec_inputs()

    def _L0_cond_setup():
        import jax, jax.numpy as jnp
        import numpy as np
        IN_FEATURES = 256
        OUT_FEATURES = 256
        BATCH = 32
        SEQ = 256
        EPS = 1e-08
        key = jax.random.key(seed)
        k1, k2, k3 = jax.random.split(key, 3)
        Efou = jax.random.normal(k1, (BATCH, SEQ, IN_FEATURES), dtype=jnp.float32)
        y = jax.random.normal(k2, (BATCH, IN_FEATURES), dtype=jnp.float32)
        weight = jax.random.normal(k3, (IN_FEATURES, OUT_FEATURES), dtype=jnp.float32)
        return {'Efou': Efou, 'y': y, 'weight': weight}
    _L0_cond_all = _L0_cond_setup()
    _L0_cond_in = {k: v for k, v in _L0_cond_all.items() if k in ('weight',)}
    del _L0_cond_all

    def _L0_ffn_setup():
        import jax, jax.numpy as jnp
        import numpy as np
        B, S, D = (4, 512, 256)
        EXP = 4
        H = EXP * D
        E = 8
        TOP_K = 2
        key = jax.random.key(seed)
        ks = jax.random.split(key, 8)
        scale1 = 1.0 / np.sqrt(D)
        scale2 = 1.0 / np.sqrt(H)
        x = jax.random.normal(ks[0], (B, S, D), dtype=jnp.float32)
        W1 = jax.random.uniform(ks[1], (E, D, H), jnp.float32, -scale1, scale1)
        b1 = jax.random.uniform(ks[2], (E, H), jnp.float32, -scale1, scale1)
        W2 = jax.random.uniform(ks[3], (E, H, D), jnp.float32, -scale2, scale2)
        b2 = jax.random.uniform(ks[4], (E, D), jnp.float32, -scale2, scale2)
        Wr = jax.random.uniform(ks[5], (D, E), jnp.float32, -scale1, scale1)
        br = jax.random.uniform(ks[6], (E,), jnp.float32, -scale1, scale1)
        return {'input_emb': x, 'W1': W1, 'b1': b1, 'W2': W2, 'b2': b2, 'Wr': Wr, 'br': br}
    _L0_ffn_all = _L0_ffn_setup()
    _L0_ffn_in = {k: v for k, v in _L0_ffn_all.items() if k in ('W1', 'b1', 'W2', 'b2', 'Wr', 'br')}
    del _L0_ffn_all
    return {'x': x, 'cond_1024': cond_1024, 'L0_cond_weight': _L0_cond_in['weight'], 'L0_ffn_W1': _L0_ffn_in['W1'], 'L0_ffn_b1': _L0_ffn_in['b1'], 'L0_ffn_W2': _L0_ffn_in['W2'], 'L0_ffn_b2': _L0_ffn_in['b2'], 'L0_ffn_Wr': _L0_ffn_in['Wr'], 'L0_ffn_br': _L0_ffn_in['br']}

def reference(x, cond_1024, L0_cond_weight, L0_ffn_W1, L0_ffn_b1, L0_ffn_W2, L0_ffn_b2, L0_ffn_Wr, L0_ffn_br):
    import jax
    import jax.numpy as jnp

    def _L0_cond_ref(Efou, y, weight):
        import jax, jax.numpy as jnp
        import numpy as np
        IN_FEATURES = 256
        OUT_FEATURES = 256
        BATCH = 32
        SEQ = 256
        EPS = 1e-08
        scale = 1.0 / np.sqrt(np.float32(weight.shape[0]))
        ys = y * scale
        d = jax.lax.rsqrt(jnp.einsum('bi,io->bo', ys * ys, weight * weight) + EPS)
        out = jnp.einsum('bsi,io->bso', Efou * ys[:, None, :], weight) * d[:, None, :]
        return out

    def _L0_ffn_ref(input_emb, W1, b1, W2, b2, Wr, br):
        import jax, jax.numpy as jnp
        import numpy as np
        B, S, D = (4, 512, 256)
        EXP = 4
        H = EXP * D
        E = 8
        TOP_K = 2
        logits = jnp.einsum('bsd,de->bse', input_emb, Wr) + br
        route_w = jax.nn.softmax(logits, axis=-1)
        _, topk_idx = jax.lax.top_k(route_w, TOP_K)
        mask = jax.nn.one_hot(topk_idx, E, dtype=route_w.dtype).sum(-2)
        routed = route_w * mask
        routed = routed / routed.sum(axis=-1, keepdims=True)
        h = jax.nn.relu(jnp.einsum('bsd,edh->ebsh', input_emb, W1) + b1[:, None, None, :])
        expert_out = jnp.einsum('ebsh,ehd->ebsd', h, W2) + b2[:, None, None, :]
        return jnp.einsum('bse,ebsd->bsd', routed, expert_out)
    x = x + _L0_ffn_ref(_L0_cond_ref(x, cond_1024, L0_cond_weight), L0_ffn_W1, L0_ffn_b1, L0_ffn_W2, L0_ffn_b2, L0_ffn_Wr, L0_ffn_br)
    return x

_drawn_inputs = setup_inputs


def setup_inputs(seed=0):
    import zlib

    import numpy as np

    out = dict(_drawn_inputs(seed))
    spreads = {}
    factors = {'L0_ffn_b1': 5.447, 'L0_ffn_b2': 4.419}
    for name, (base, spread) in spreads.items():
        noise = np.random.default_rng([zlib.crc32(name.encode()), seed]).standard_normal(out[name].shape)
        drawn = base * np.exp(spread * noise) if base else spread * noise
        out[name] = jnp.asarray(drawn.astype(out[name].dtype))
    for name, factor in factors.items():
        out[name] = (out[name] * factor).astype(out[name].dtype)
    return out
```

```python
import concourse.bass as bass
from concourse import mybir
from contextlib import ExitStack


def bass_adaln_moe_ffn(
    nc: bass.Bass,
    x: bass.AP,
    xT: bass.AP,
    condT: bass.AP,
    w: bass.AP,
    wT: bass.AP,
    wr: bass.AP,
    br: bass.AP,
    experts: bass.AP,
    b1: bass.AP,
    b2: bass.AP,
    slot_weight: bass.AP,
    out: bass.AP,
):
    f32 = mybir.dt.float32
    f32r = mybir.dt.float32r
    bf16 = mybir.dt.bfloat16
    i32 = mybir.dt.int32
    ALU = mybir.AluOpType
    ACT = mybir.ActivationFunctionType
    AX = mybir.AxisListType
    ds = bass.ds

    P = 128
    T, D = x.shape
    DC = D // P
    B = condT.shape[2]
    S = T // B
    ST = S // P
    NT = T // P
    E = br.shape[0]
    HC = b1.shape[2]
    NQ = experts.shape[1]
    CQ = HC // NQ
    QW = experts.shape[3]
    W1Q = DC * CQ * P
    TOPK = 2
    Q = (out.shape[0] - T) // P
    TB = Q * P
    MAXB = (TOPK * T + E * (TB - 1)) // TB
    NSC = MAXB * Q
    NJ = -(-T // TB)
    ZW = D + E
    EPS = 1e-8
    LAG = 2
    NHP = 2
    NHX = 4
    U = 8
    XG = 2
    NX = 4
    GT = U * ST
    NG = NT // GT
    NR = 17
    JW = 2 * E * 2
    TG = P // JW
    NTG = NT // TG
    HOT = 4
    INIT = 8

    z_rows = nc.dram_tensor("z_rows", (T + TB, ZW), f32, kind="Internal").ap()
    d_rows = nc.dram_tensor("d_rows", (B, ZW), f32, kind="Internal").ap()

    ctx = ExitStack()
    with ctx:
        def sb(name, shape, dt, stack=ctx):
            return stack.enter_context(nc.sbuf_tensor(name, shape, dt))

        def sem(name):
            return ctx.enter_context(nc.semaphore(name))

        idx_all = sb("idx_all", [P, NSC + Q], i32)
        block_expert = sb("block_expert", [P, MAXB + 1], i32)
        idx_get = sb("idx_get", [P, Q], i32)
        idx_put = sb("idx_put", [P, Q], i32)
        n_blocks = sb("n_blocks", [P, 2], i32)
        b1_all = sb("b1_all", [P, E, HC], f32)
        b2_all = sb("b2_all", [P, E, D], f32)
        ident = sb("ident", [P, P], f32)
        zero = sb("zero", [P, ZW], f32)
        raw = [sb(f"raw{k}", [P, QW], f32) for k in range(NQ)]

        cond_sb = sb("cond_sb", [P, DC, B], f32)
        ys = sb("ys", [P, DC, B], f32)
        ys2 = sb("ys2", [P, DC, B], f32)
        w_sb = sb("w_sb", [P, DC, D], f32)
        wT_sb = sb("wT_sb", [P, DC, D], f32)
        w2_sb = sb("w2_sb", [P, DC, D], f32)
        wr_sb = sb("wr_sb", [P, DC, E], f32)
        v = sb("v", [P, DC, B], f32)
        root = sb("root", [P, DC, B], f32)
        rough = sb("rough", [P, DC, B], f32)
        fix = sb("fix", [P, DC, B], f32)
        dT = sb("dT", [P, DC, B], f32)
        dwr = sb("dwr", [P, DC, B, E], f32)
        m_all = sb("m_all", [P, 2, DC, B * E], f32r)
        d_sb = sb("d_sb", [B, ZW], f32)

        br_rep = sb("br_rep", [P, E], f32)
        logit = sb("logit", [P, GT, E], f32)
        tie = sb("tie", [P, GT, E], f32)
        top = sb("top", [P, GT], f32)
        inv = sb("inv", [P, GT], f32)
        prob = sb("prob", [P, NT, E], f32)
        first = sb("first", [P, NT, E], f32)
        second = sb("second", [P, NT, E], f32)
        both = sb("both", [P, NT, E], f32)
        kept = sb("kept", [P, NT, E], f32)
        kept_sum = sb("kept_sum", [P, NT], f32)
        kept_inv = sb("kept_inv", [P, NT], f32)
        prefer = sb("prefer", [P, E], f32)
        chosen = sb("chosen", [P, NT, E], bf16)
        before = sb("before", [P, P], bf16)
        ones_bf = sb("ones_bf", [P, P], bf16)
        ident_bf = sb("ident_bf", [P, P], bf16)
        ones = sb("ones", [P, E * NT], f32)
        start_e = sb("start_e", [P, E], f32)
        count_e = sb("count_e", [P, E], f32)
        nb_e = sb("nb_e", [P, E], f32)
        nb_end = sb("nb_end", [P, E], f32)
        col_e = sb("col_e", [P, E], f32)
        steps = sb("steps", [P, NJ], f32)
        more = sb("more", [P, E, NJ], f32)
        blocks = sb("blocks", [P, MAXB + 1], f32)
        past = sb("past", [P, MAXB + 1, E], f32)
        ended = sb("ended", [P, MAXB + 1], f32)
        place = sb("place", [P, TOPK, NT], f32)
        over = sb("over", [P, TOPK, NT], f32)
        row = sb("row", [P, TOPK, NT], bf16)
        row_no = sb("row_no", [P, 1], f32)
        iota_row = sb("iota_row", [P, P], bf16)
        iota_col = sb("iota_col", [P, NSC], f32)
        weight_j = sb("weight_j", [P, NTG], f32)
        col_j = sb("col_j", [P, NTG], f32)
        spare = sb("spare", [P, NSC + Q], f32)
        free_id = sb("free_id", [P, NSC], f32)
        z_all = sb("z_all", [P, NT, ZW], f32)

        stage_a = ExitStack()
        d_rep = sb("d_rep", [P, B, ZW], f32, stage_a)
        x_buf = sb("x_buf", [P, U // XG, DC, XG * S], f32, stage_a)
        x_s = [sb(f"x_s{u}", [P, DC, S], f32, stage_a) for u in range(2)]
        x_hi = [sb(f"x_hi{u}", [P, DC, S], f32r, stage_a) for u in range(NX)]
        x_lo = [sb(f"x_lo{u}", [P, DC, S], f32r, stage_a) for u in range(NX)]
        w_m = [sb(f"w_m{u}", [P, 2, DC, ZW], f32r, stage_a) for u in range(2)]
        stage_a.close()
        stage_b = ExitStack()
        w_hi = [sb(f"w_hi{k}", [P, QW], f32r, stage_b) for k in range(NQ)]
        w_lo = [sb(f"w_lo{k}", [P, QW], f32r, stage_b) for k in range(NQ)]
        stage_r = ExitStack()
        per_tile = sb("per_tile", [P, E * NT], f32, stage_r)
        seen = sb("seen", [P, E * NT], f32, stage_r)
        seen_i = sb("seen_i", [P, E * NT], i32, stage_r)
        col_i = sb("col_i", [P, E * NT], i32, stage_r)
        rest_i = sb("rest_i", [P, E * NT], i32, stage_r)
        rank = sb("rank", [P, NT, E], f32, stage_r)
        mine = [sb(f"mine{k}", [P, NT, E], f32, stage_r) for k in range(TOPK)]
        hot = sb("hot", [P, TOPK, NT, 2, E, 2], bf16, stage_r)
        col_of = sb("col_of", [P, NT, 2, E, 2], bf16, stage_r)
        row_hot = [sb(f"row_hot{g}", [P, TG, TOPK, P], bf16, stage_r) for g in range(HOT)]
        col_hot = sb("col_hot", [P, NTG, NSC], bf16, stage_r)
        partial = sb("partial", [P, NTG * P], bf16, stage_r)
        stage_r.close()
        h = [sb(f"h{i}", [P, TB], f32, stage_b) for i in range(NHP)]
        h_hi = [sb(f"h_hi{i}", [P, TB], f32r, stage_b) for i in range(NHX)]
        h_lo = [sb(f"h_lo{i}", [P, TB], f32r, stage_b) for i in range(NHX)]
        z_row = sb("z_row", [P, Q, ZW], f32, stage_b)
        z_hi = sb("z_hi", [P, DC, TB], f32r, stage_b)
        z_lo = sb("z_lo", [P, DC, TB], f32r, stage_b)
        y = sb("y", [P, Q, D], f32, stage_b)
        b2_r = sb("b2_r", [P, Q, D], f32, stage_b)
        r_next = sb("r_next", [P, Q], f32, stage_b)
        r_cur = sb("r_cur", [P, Q], f32, stage_b)
        stage_b.close()

        psum = ctx.enter_context(nc.psum_tensor("psum", [P, 8, 512], f32))
        bank = [psum[:, i, :] for i in range(8)]
        d_ps, dr_ps = bank[0], bank[1]
        m_ps = [bank[2 + c] for c in range(DC)]
        z_ps = [psum[:, 4 + ST * u:4 + ST * (u + 1), 0:ZW] for u in range(2)]
        rank_ps, total_ps, table_ps, col_ps = bank[0], bank[1], bank[2], bank[3]
        BG = 512 // P
        part_ps = [bank[4 + i] for i in range(NTG // BG)]
        h_ps = [bank[i] for i in range(NHP)]
        y_ps = [bank[NHP + q] for q in range(Q)]
        zt_ps = [bank[NHP + Q + c] for c in range(DC)]

        s_in = sem("s_in")
        s_bias = sem("s_bias")
        s_const = sem("s_const")
        s_ys = sem("s_ys")
        s_sum = sem("s_sum")
        s_v = sem("s_v")
        s_root = sem("s_root")
        s_d = sem("s_d")
        s_dr = sem("s_dr")
        s_m = sem("s_m")
        s_drow = sem("s_drow")
        s_dst = sem("s_dst")
        s_drep = [sem(f"s_drep{g}") for g in range(NG)]
        s_w = sem("s_w")
        s_x = [sem(f"s_x{g}") for g in range(U // XG)]
        s_xs = sem("s_xs")
        s_xhi = sem("s_xhi")
        s_xlo = sem("s_xlo")
        s_wm = sem("s_wm")
        s_zps = sem("s_zps")
        s_z = sem("s_z")
        s_route = sem("s_route")
        s_exp = sem("s_exp")
        s_chosen = sem("s_chosen")
        s_kept = sem("s_kept")
        s_routed = sem("s_routed")
        s_zst = sem("s_zst")
        s_init = sem("s_init")
        s_rank = sem("s_rank")
        s_place = sem("s_place")
        s_colof = sem("s_colof")
        s_colps = sem("s_colps")
        s_colj = sem("s_colj")
        s_colhot = sem("s_colhot")
        s_hot = sem("s_hot")
        s_hot2 = sem("s_hot2")
        s_rowhot = sem("s_rowhot")
        s_part = sem("s_part")
        s_psb = sem("s_psb")
        s_tab = sem("s_tab")
        s_dec = sem("s_dec")
        s_blocks = sem("s_blocks")
        s_idx = sem("s_idx")
        s_raw = [sem(f"s_raw{k}") for k in range(NQ)]
        s_whi = sem("s_whi")
        s_wlo = sem("s_wlo")
        s_idxg0 = sem("s_idxg0")
        s_idxg = sem("s_idxg")
        s_idxp = sem("s_idxp")
        s_get = sem("s_get")
        s_put = sem("s_put")
        s_zt = sem("s_zt")
        s_zhi = sem("s_zhi")
        s_zlo = sem("s_zlo")
        s_rnext = sem("s_rnext")
        s_rcur = sem("s_rcur")
        s_b2r = sem("s_b2r")
        s_h1 = sem("s_h1")
        s_relu = sem("s_relu")
        s_hhi = sem("s_hhi")
        s_hlo = sem("s_hlo")
        s_h2 = sem("s_h2")
        s_y = sem("s_y")

        N_CONST = 17
        N_INPUTS = 4
        N_BIAS = 4
        N_BLOCKS = 3

        def blocks_of(eng):
            eng.wait_ge(s_blocks, N_BLOCKS)
            return eng.value_load(n_blocks[0:1, 0:1], min_val=2, max_val=MAXB)

        def last_of(eng):
            return eng.value_load(n_blocks[0:1, 1:2], min_val=1, max_val=MAXB - 1)

        def expert_of(eng, b):
            return eng.value_load(block_expert[0:1, ds(b, 1)], min_val=0, max_val=E - 1)

        block = ctx.enter_context(nc.Block())

        @block.sync
        def _(sp):
            sp.dma_start(cond_sb[:], condT).then_inc(s_in, 16)
            sp.dma_start(w_sb[:], w.rearrange("(c p) o -> p c o", p=P)).then_inc(s_in, 16)
            sp.dma_start(wT_sb[:], wT.rearrange("(c p) i -> p c i", p=P)).then_inc(s_in, 16)
            sp.dma_start(wr_sb[:], wr.rearrange("(c p) e -> p c e", p=P)).then_inc(s_in, 16)
            for g in range(U // XG):
                sp.dma_start(x_buf[:, g], xT[:, :, g * XG * S:(g + 1) * XG * S]).then_inc(s_x[g], 16)

            def copy_x(i):
                rows = T // INIT
                sp.dma_start(out[ds(i * rows, rows), :], x[ds(i * rows, rows), :]).then_inc(s_init, 16)

            copy_x(NG)
            sp.wait_ge(s_drow, 2)
            sp.dma_start(d_rows, d_sb[:]).then_inc(s_dst, 16)
            sp.wait_ge(s_dst, 16)
            for g in range(NG):
                sp.dma_start(d_rep[:, g * U:(g + 1) * U, :].rearrange("p b z -> p (b z)"),
                             d_rows[g * U:(g + 1) * U, :].rearrange("(a b) z -> a (b z)", a=1)
                             .to_broadcast([P, U * ZW])).then_inc(s_drep[g], 16)
            sp.dma_start(b1_all[:], b1).then_inc(s_bias, 16)
            sp.dma_start(weight_j[:], slot_weight).then_inc(s_bias, 16)
            sp.dma_start(br_rep[:], br.rearrange("(a e) -> a e", a=1).to_broadcast([P, E])).then_inc(s_bias, 16)
            sp.dma_start(b2_all[:].rearrange("p e d -> p (e d)"),
                         b2.rearrange("(a e) d -> a (e d)", a=1).to_broadcast([P, E * D])).then_inc(s_bias, 16)
            copy_x(0)
            with sp.Fori(1, NG) as i:
                for g in range(U // XG):
                    sp.wait_ge(s_xs, ((i - 1) * U + (g + 1) * XG) * DC)
                    sp.dma_start(x_buf[:, g], xT[:, :, ds((i * U + g * XG) * S, XG * S)]).then_inc(s_x[g], 16)
                copy_x(i)
            sp.wait_ge(s_const, N_CONST)
            for q in range(Q):
                sp.dma_start(z_rows[T + q * P:T + (q + 1) * P, :], zero[:]).then_inc(s_zst, 16)
            sp.wait_ge(s_routed, 1)
            sp.dma_start(z_rows[0:T, :].rearrange("(n p) z -> p n z", p=P), z_all[:]).then_inc(s_zst, 16)
            n = blocks_of(sp)

            def load_weights(b, k, e):
                sp.dma_start(raw[k][:], experts[ds(e, 1), k].rearrange("a p n -> (a p) n")).then_inc(s_raw[k], 16)

            e = expert_of(sp, 0)
            for k in range(NQ):
                load_weights(0, k, e)
            sp.wait_ge(s_get, 16 * Q)
            for i in range(NG + 1, INIT):
                copy_x(i)
            with sp.Fori(0, n) as b:
                e = expert_of(sp, b + 1)
                for k in range(NQ):
                    sp.wait_ge(s_wlo, b * NQ + k + 1)
                    load_weights(b + 1, k, e)
            sp.wait_ge(s_init, INIT * 16)

        @block.gpsimd
        def _(pool):
            exact = dict(allow_small_or_imprecise_dtypes=True)
            pool.memset(ident[:], 0.0).then_inc(s_const, 1)
            pool.memset(before[:], 0.0).then_inc(s_const, 1)
            pool.memset(ones_bf[:], 1.0).then_inc(s_const, 1)
            pool.memset(ones[:], 1.0).then_inc(s_const, 1)
            pool.memset(zero[:], 0.0).then_inc(s_const, 1)
            pool.memset(ident_bf[:], 0.0).then_inc(s_const, 1)
            pool.memset(d_sb[:], 1.0).then_inc(s_const, 1)
            pool.wait_ge(s_const, 7)
            pool.affine_select(out=ident[:], in_=ident[:], compare_op=ALU.not_equal, fill=1.0, base=0,
                               pattern=[[-1, P]], channel_multiplier=1).then_inc(s_const, 1)
            pool.affine_select(out=ident_bf[:], in_=ident_bf[:], compare_op=ALU.not_equal, fill=1.0, base=0,
                               pattern=[[-1, P]], channel_multiplier=1).then_inc(s_const, 1)
            pool.affine_select(out=before[:], in_=before[:], compare_op=ALU.is_ge, fill=1.0, base=0,
                               pattern=[[-1, P]], channel_multiplier=1).then_inc(s_const, 1)
            pool.iota(prefer[:], pattern=[[-1, E]], base=E, channel_multiplier=0, **exact).then_inc(s_const, 1)
            pool.iota(steps[:], pattern=[[TB, NJ]], base=0, channel_multiplier=0, **exact).then_inc(s_const, 1)
            pool.iota(blocks[:], pattern=[[1, MAXB + 1]], base=0, channel_multiplier=0, **exact).then_inc(s_const, 1)
            pool.iota(iota_row[:], pattern=[[1, P]], base=0, channel_multiplier=0, **exact).then_inc(s_const, 1)
            pool.iota(iota_col[:], pattern=[[1, NSC]], base=0, channel_multiplier=0, **exact).then_inc(s_const, 1)
            pool.iota(row_no[:], pattern=[[0, 1]], base=1, channel_multiplier=1, **exact).then_inc(s_const, 1)
            pool.iota(spare[:].rearrange("p (b q) -> p b q", q=Q), pattern=[[0, MAXB + 1], [P, Q]],
                      base=T + 1, channel_multiplier=1, **exact).then_inc(s_const, 1)

            pool.wait_ge(s_const, N_CONST)
            for q in range(Q):
                pool.dma_start(out[T + q * P:T + (q + 1) * P, :], zero[:, 0:D]).then_inc(s_put, 16)

            def x_lo_of(u, b):
                pool.wait_ge(s_xhi, b + 1)
                pool.tensor_tensor(out=x_lo[u % NX][:], in0=x_s[u % 2][:], in1=x_hi[u % NX][:].bitcast(f32),
                                   op=ALU.subtract).then_inc(s_xlo, 1)

            def router_columns(u, b, fresh):
                if not fresh:
                    pool.wait_ge(s_zps, b - 1)
                pool.tensor_copy(w_m[u % 2][:, :, :, D:ZW], m_all[:, :, :, ds(b * E, E)]).then_inc(s_wm, 1)

            pool.wait_ge(s_w, 6 * DC)
            for u in range(U):
                x_lo_of(u, u)
                router_columns(u, u, u < 2)
            with pool.Fori(1, NG) as i:
                for u in range(U):
                    x_lo_of(u, i * U + u)
                    router_columns(u, i * U + u, False)

            pool.wait_ge(s_colj, 1)
            for g in range(NTG):
                pool.tensor_scalar(col_hot[:, g, :], iota_col[:], col_j[:, g:g + 1], weight_j[:, g:g + 1],
                                   ALU.is_equal, ALU.mult).then_inc(s_colhot, 1)

            n = blocks_of(pool)
            pool.wait_ge(s_idx, 2)

            def gather(b, copied, count, constant):
                pool.tensor_copy(idx_get[:], idx_all[:, ds(b * Q, Q)]).then_inc(copied, 1)
                pool.wait_ge(*constant)
                pool.wait_ge(copied, count)
                for q in range(Q):
                    pool.indirect_dma_start(
                        out=z_row[:, q, :], out_offset=None, in_=z_rows,
                        in_offset=bass.IndirectOffsetOnAxis(ap=idx_get[:, q:q + 1], axis=0)).then_inc(s_get, 16)

            def row_free(b):
                pool.wait_ge(s_zt, b + 1)
                pool.wait_ge(s_rnext, b + 1)

            def scatter_add(b):
                pool.tensor_copy(idx_put[:], idx_all[:, ds(b * Q, Q)]).then_inc(s_idxp, 1)
                pool.wait_ge(s_init, INIT * 16)
                pool.wait_ge(s_idxp, b + 1)
                for q in range(Q):
                    pool.indirect_dma_start(
                        out=out, out_offset=bass.IndirectOffsetOnAxis(ap=idx_put[:, q:q + 1], axis=0),
                        in_=y[:, q, :], in_offset=None, compute_op=ALU.add).then_inc(s_put, 16)

            rows_stored = (s_zst, (1 + Q) * 16)
            gather(0, s_idxg0, 1, rows_stored)
            row_free(0)
            gather(1, s_idxg0, 2, rows_stored)
            with pool.Fori(1, n) as b:
                row_free(b)
                gather(b + 1, s_idxg, b, (s_routed, 1))
                pool.wait_ge(s_y, b * Q)
                pool.wait_ge(s_put, b * (16 * Q))
                scatter_add(b - 1)
            last = last_of(pool)
            pool.wait_ge(s_y, (last + 1) * Q)
            pool.wait_ge(s_put, (last + 1) * (16 * Q))
            scatter_add(last)
            for k in range(NQ):
                pool.wait_ge(s_raw[k], (last + 2) * 16)
            pool.wait_ge(s_put, (last + 2) * (16 * Q))

        @block.scalar
        def _(act):
            act.wait_ge(s_v, 1)
            act.activation(root[:], v[:], ACT.Sqrt).then_inc(s_root, 1)

            def x_hi_of(u, i, b):
                if u % XG == 0:
                    act.wait_ge(s_x[u // XG], (i + 1) * 16)
                for c in range(DC):
                    act.activation(x_s[u % 2][:, c, :], x_buf[:, u // XG, c, (u % XG) * S:(u % XG + 1) * S],
                                   ACT.Copy, scale=ys[:, c, ds(b, 1)]).then_inc(s_xs, 1)
                act.wait_ge(s_xs, (b + 1) * DC)
                act.activation(x_hi[u % NX][:], x_s[u % 2][:], ACT.Copy).then_inc(s_xhi, 1)

            def softmax_exp(g):
                act.wait_ge(s_route, g * NR + 3)
                act.activation(prob[:, ds(g * GT, GT), :], logit[:], ACT.Exp).then_inc(s_exp, 1)

            act.wait_ge(s_ys, 1)
            for u in range(U):
                if u >= NX:
                    act.wait_ge(s_zps, u - NX + 1)
                if u >= 2:
                    act.wait_ge(s_xlo, u - 1)
                x_hi_of(u, 0, u)
            with act.Fori(1, NG) as i:
                for u in range(U):
                    act.wait_ge(s_zps, i * U + u - NX + 1)
                    act.wait_ge(s_xlo, i * U + u - 1)
                    x_hi_of(u, i, i * U + u)
                    if u == 4:
                        softmax_exp(i - 1)
            softmax_exp(NG - 1)

            for k in range(TOPK):
                act.wait_ge(s_hot, 2 * (k + 1))
                act.activation(hot[:, k, :, 1], hot[:, k, :, 0], ACT.Copy, scale=row_no[:, 0:1]).then_inc(s_hot2, 1)
            act.wait_ge(s_colps, 1)
            act.activation(col_j[:], col_ps[:, 0:NTG], ACT.Copy).then_inc(s_colj, 1)
            for i in range(NTG // BG):
                act.wait_ge(s_part, (i + 1) * BG)
                act.activation(partial[:, i * 512:(i + 1) * 512], part_ps[i], ACT.Copy).then_inc(s_psb, 1)

            n = blocks_of(act)
            act.wait_ge(s_bias, N_BIAS * 16)

            def weights_hi(b, k, fresh):
                act.wait_ge(s_raw[k], b * 16 + 16)
                if not fresh:
                    act.wait_ge(s_h2, (b - 1) * HC + (k + 1) * CQ)
                act.activation(w_hi[k][:], raw[k][:], ACT.Copy).then_inc(s_whi, 1)

            def z_hi_of(b, fresh):
                act.wait_ge(s_zt, b + 1)
                if not fresh:
                    act.wait_ge(s_h1, b * HC)
                for c in range(DC):
                    act.activation(z_hi[:, c, :], zt_ps[c][:, 0:TB], ACT.Copy).then_inc(s_zhi, 1)

            def block_of_act(b, fresh):
                e = expert_of(act, b)
                for c in range(HC):
                    act.wait_ge(s_h1, b * HC + c + 1)
                    if not (fresh and c < NHP):
                        act.wait_ge(s_hlo, b * HC + c + 1 - NHP)
                    act.activation(h[c % NHP][:], h_ps[c % NHP][:, 0:TB], ACT.Relu,
                                   bias=b1_all[:, ds(e, 1), c]).then_inc(s_relu, 1)
                    if c == 0:
                        weights_hi(b, 2, fresh)
                    if c == 1:
                        act.wait_ge(s_rcur, b + 1)
                        for q in range(Q):
                            act.activation(b2_r[:, q, :], b2_all[:, ds(e, 1), :].rearrange("p a d -> p (a d)"),
                                           ACT.Copy, scale=r_cur[:, q:q + 1]).then_inc(s_b2r, 1)
                    if c == 2:
                        weights_hi(b, 3, fresh)
                    if c == 4:
                        weights_hi(b + 1, 0, False)
                    if c == 6:
                        weights_hi(b + 1, 1, False)
                z_hi_of(b + 1, False)

            weights_hi(0, 0, True)
            weights_hi(0, 1, True)
            z_hi_of(0, True)
            block_of_act(0, True)
            with act.Fori(1, n) as b:
                block_of_act(b, False)

        @block.vector
        def _(dve):
            done = {}

            def step(ins, s):
                done[s.name] = done.get(s.name, 0) + 1
                ins.then_inc(s, 1)
                dve.wait_ge(s, done[s.name])

            dve.wait_ge(s_in, N_INPUTS * 16)
            step(dve.tensor_scalar(ys[:], cond_sb[:], float(D) ** -0.5, None, ALU.mult), s_ys)
            dve.tensor_tensor(out=ys2[:], in0=ys[:], in1=ys[:], op=ALU.mult).then_inc(s_ys, 1)
            dve.tensor_tensor(out=w2_sb[:], in0=w_sb[:], in1=w_sb[:], op=ALU.mult).then_inc(s_ys, 1)
            for c in range(DC):
                for u in range(2):
                    dve.tensor_copy(w_m[u][:, 0, c, 0:D], w_sb[:, c, :]).then_inc(s_w, 1)
            dve.wait_ge(s_w, 2 * DC)
            for c in range(DC):
                for u in range(2):
                    dve.tensor_tensor(out=w_m[u][:, 1, c, 0:D], in0=w_sb[:, c, :],
                                      in1=w_m[u][:, 0, c, 0:D].bitcast(f32), op=ALU.subtract).then_inc(s_w, 1)
            dve.wait_ge(s_sum, 1)
            step(dve.tensor_scalar(v[:], d_ps[:, 0:DC * B].rearrange("p (c b) -> p c b", c=DC), EPS, None, ALU.add), s_v)
            dve.wait_ge(s_root, 1)
            step(dve.reciprocal(rough[:], root[:]), s_d)
            step(dve.tensor_tensor(out=fix[:], in0=rough[:], in1=rough[:], op=ALU.mult), s_d)
            step(dve.tensor_tensor(out=fix[:], in0=fix[:], in1=v[:], op=ALU.mult), s_d)
            step(dve.tensor_scalar(fix[:], fix[:], -0.5, 1.5, ALU.mult, ALU.add), s_d)
            step(dve.tensor_tensor(out=dT[:], in0=fix[:], in1=rough[:], op=ALU.mult), s_d)
            dve.tensor_tensor(out=dwr[:], in0=dT[:].unsqueeze(3).to_broadcast([P, DC, B, E]),
                              in1=wr_sb[:].unsqueeze(2).to_broadcast([P, DC, B, E]), op=ALU.mult).then_inc(s_d, 1)
            dve.wait_ge(s_dr, 1)
            dve.wait_ge(s_const, N_CONST)
            for c in range(DC):
                dve.tensor_copy(d_sb[:, c * P:(c + 1) * P], dr_ps[0:B, c * P:(c + 1) * P]).then_inc(s_drow, 1)
            dve.wait_ge(s_m, 1)
            for c in range(DC):
                dve.tensor_copy(m_all[:, 0, c, :], m_ps[c][:, 0:B * E]).then_inc(s_w, 1)
            dve.wait_ge(s_w, 5 * DC)
            for c in range(DC):
                dve.tensor_tensor(out=m_all[:, 1, c, :], in0=m_ps[c][:, 0:B * E],
                                  in1=m_all[:, 0, c, :].bitcast(f32), op=ALU.subtract).then_inc(s_w, 1)
            dve.wait_ge(s_w, 6 * DC)

            def z_of(u, b):
                dve.wait_ge(s_zps, b + 1)
                dve.tensor_tensor(out=z_all[:, ds(b * ST, ST), :], in0=z_ps[u % 2],
                                  in1=d_rep[:, ds(b, 1), :].to_broadcast([P, ST, ZW]), op=ALU.mult).then_inc(s_z, 1)

            def over_e(a):
                return a[:].unsqueeze(2).to_broadcast([P, GT, E])

            def route(u, g):
                tiles = ds(g * GT, GT)
                p_g, first_g, second_g = prob[:, tiles, :], first[:, tiles, :], second[:, tiles, :]
                prefer_g = prefer[:].unsqueeze(1).to_broadcast([P, GT, E])

                def step(n, ins):
                    ins.then_inc(s_route, 1)
                    dve.wait_ge(s_route, g * NR + n)

                if u == 0:
                    dve.wait_ge(s_z, (g + 1) * U)
                    step(1, dve.tensor_tensor(out=logit[:], in0=z_all[:, tiles, D:ZW],
                                              in1=br_rep[:].unsqueeze(1).to_broadcast([P, GT, E]), op=ALU.add))
                    step(2, dve.tensor_reduce(top[:], logit[:], AX.X, ALU.max))
                if u == 1:
                    step(3, dve.tensor_tensor(out=logit[:], in0=logit[:], in1=over_e(top), op=ALU.subtract))
                if u == 4:
                    dve.wait_ge(s_exp, g + 1)
                    step(4, dve.tensor_reduce(top[:], p_g, AX.X, ALU.add))
                    step(5, dve.reciprocal(inv[:], top[:]))
                    step(6, dve.tensor_tensor(out=p_g, in0=p_g, in1=over_e(inv), op=ALU.mult))
                if u == 5:
                    step(7, dve.tensor_reduce(top[:], p_g, AX.X, ALU.max))
                    step(8, dve.tensor_tensor(out=tie[:], in0=p_g, in1=over_e(top), op=ALU.is_equal))
                    step(9, dve.tensor_tensor(out=tie[:], in0=tie[:], in1=prefer_g, op=ALU.mult))
                    step(10, dve.tensor_reduce(top[:], tie[:], AX.X, ALU.max))
                if u == 6:
                    step(11, dve.tensor_tensor(out=first_g, in0=tie[:], in1=over_e(top), op=ALU.is_equal))
                    step(12, dve.scalar_tensor_tensor(out=logit[:], in0=first_g, scalar=-4.0, in1=p_g,
                                                      op0=ALU.mult, op1=ALU.add))
                    step(13, dve.tensor_reduce(top[:], logit[:], AX.X, ALU.max))
                    step(14, dve.tensor_tensor(out=tie[:], in0=logit[:], in1=over_e(top), op=ALU.is_equal))
                if u == 7:
                    step(15, dve.tensor_tensor(out=tie[:], in0=tie[:], in1=prefer_g, op=ALU.mult))
                    step(16, dve.tensor_reduce(top[:], tie[:], AX.X, ALU.max))
                    step(17, dve.tensor_tensor(out=second_g, in0=tie[:], in1=over_e(top), op=ALU.is_equal))
                    dve.tensor_tensor(out=chosen[:, tiles, :], in0=first_g, in1=second_g, op=ALU.add).then_inc(s_chosen, 1)

            dve.wait_ge(s_drep[0], 16)
            for u in range(U):
                z_of(u, u)
            for g in range(NG):
                dve.wait_ge(s_drep[g], 16)
            dve.wait_ge(s_bias, N_BIAS * 16)
            with dve.Fori(1, NG) as i:
                for u in range(U):
                    z_of(u, i * U + u)
                    route(u, i - 1)
            for u in range(U):
                route(u, NG - 1)

            step(dve.tensor_tensor(out=both[:], in0=first[:], in1=second[:], op=ALU.add), s_kept)
            step(dve.tensor_tensor(out=kept[:], in0=prob[:], in1=both[:], op=ALU.mult), s_kept)
            step(dve.tensor_reduce(kept_sum[:], kept[:], AX.X, ALU.add), s_kept)
            step(dve.reciprocal(kept_inv[:], kept_sum[:]), s_kept)
            dve.tensor_tensor(out=z_all[:, :, D:ZW], in0=kept[:],
                              in1=kept_inv[:].unsqueeze(2).to_broadcast([P, NT, E]), op=ALU.mult).then_inc(s_routed, 1)

            def e_major(a):
                return a[:].rearrange("p (e n) -> p e n", e=E)

            def by_tile(a):
                return a[:].rearrange("p (e n) -> p n e", e=E)

            dve.wait_ge(s_rank, 2)
            step(dve.tensor_copy(e_major(per_tile), total_ps[:, 0:NT * E].rearrange("p (n e) -> p e n", e=E)), s_place)
            step(dve.tensor_tensor_scan(seen[:], ones[:], per_tile[:], 0.0, ALU.mult, ALU.add), s_place)
            step(dve.tensor_tensor(out=per_tile[:], in0=seen[:], in1=per_tile[:], op=ALU.subtract), s_place)
            step(dve.tensor_copy(start_e[:], e_major(per_tile)[:, :, 0]), s_place)
            dve.tensor_tensor(out=count_e[:], in0=e_major(seen)[:, :, NT - 1], in1=start_e[:],
                              op=ALU.subtract).then_inc(s_place, 1)
            done[s_place.name] += 1
            step(dve.tensor_tensor(out=e_major(seen_i), in0=e_major(per_tile),
                                   in1=start_e[:].unsqueeze(2).to_broadcast([P, E, NT]), op=ALU.subtract), s_place)
            step(dve.tensor_single_scalar(rest_i[:], seen_i[:], P - 1, op=ALU.bitwise_and), s_place)
            dve.tensor_single_scalar(col_i[:], seen_i[:], P.bit_length() - 1,
                                     op=ALU.logical_shift_right).then_inc(s_place, 1)
            done[s_place.name] += 1
            step(dve.tensor_tensor(out=rank[:], in0=rank_ps[:, 0:NT * E].rearrange("p (n e) -> p n e", e=E),
                                   in1=by_tile(rest_i), op=ALU.add), s_place)
            for k, best in enumerate((first, second)):
                step(dve.tensor_tensor(out=mine[k][:], in0=best[:], in1=rank[:], op=ALU.mult), s_place)
                step(dve.tensor_reduce(place[:, k, :], mine[k][:], AX.X, ALU.add), s_place)
            step(dve.tensor_scalar(over[:], place[:], float(P), None, ALU.is_ge), s_place)
            step(dve.scalar_tensor_tensor(out=row[:], in0=over[:], scalar=-float(P), in1=place[:],
                                          op0=ALU.mult, op1=ALU.add), s_place)
            for k, best in enumerate((first, second)):
                dve.tensor_tensor(out=hot[:, k, :, 0, :, 1], in0=best[:],
                                  in1=over[:, k, :].unsqueeze(2).to_broadcast([P, NT, E]), op=ALU.mult).then_inc(s_hot, 1)
                dve.wait_ge(s_hot, 2 * k + 1)
                dve.tensor_tensor(out=hot[:, k, :, 0, :, 0], in0=best[:], in1=hot[:, k, :, 0, :, 1],
                                  op=ALU.subtract).then_inc(s_hot, 1)

            step(dve.tensor_tensor(out=more[:], in0=count_e[:].unsqueeze(2).to_broadcast([P, E, NJ]),
                                   in1=steps[:].unsqueeze(1).to_broadcast([P, E, NJ]), op=ALU.is_gt), s_place)
            step(dve.tensor_reduce(nb_e[:], more[:], AX.X, ALU.add), s_place)
            step(dve.tensor_tensor_scan(nb_end[:], ones[:, 0:E], nb_e[:], 0.0, ALU.mult, ALU.add), s_place)
            dve.tensor_copy(n_blocks[:, 0:1], nb_end[:, E - 1:E]).then_inc(s_blocks, 1)
            dve.tensor_scalar(n_blocks[:, 1:2], nb_end[:, E - 1:E], -1.0, None, ALU.add).then_inc(s_blocks, 1)
            step(dve.tensor_tensor(out=past[:], in0=blocks[:].unsqueeze(2).to_broadcast([P, MAXB + 1, E]),
                                   in1=nb_end[:].unsqueeze(1).to_broadcast([P, MAXB + 1, E]), op=ALU.is_ge), s_place)
            step(dve.tensor_reduce(ended[:], past[:], AX.X, ALU.add), s_place)
            dve.tensor_scalar(block_expert[:], ended[:], float(E - 1), None, ALU.min).then_inc(s_blocks, 1)
            step(dve.tensor_tensor(out=col_e[:], in0=nb_end[:], in1=nb_e[:], op=ALU.subtract), s_place)
            step(dve.scalar_tensor_tensor(out=e_major(seen), in0=col_e[:].unsqueeze(2).to_broadcast([P, E, NT]),
                                          scalar=float(Q), in1=e_major(col_i), op0=ALU.mult, op1=ALU.add), s_place)
            for half in range(2):
                for o in range(2):
                    dve.tensor_scalar(col_of[:, :, half, :, o], by_tile(seen), float(o), None,
                                      ALU.add).then_inc(s_colof, 1)

            for g in range(NTG):
                if g >= HOT:
                    dve.wait_ge(s_part, g - HOT + 1)
                dve.tensor_tensor(out=row_hot[g % HOT][:].rearrange("p t k r -> p k t r"),
                                  in0=iota_row[:].unsqueeze(1).unsqueeze(1).to_broadcast([P, TOPK, TG, P]),
                                  in1=row[:, :, g * TG:(g + 1) * TG].unsqueeze(3).to_broadcast([P, TOPK, TG, P]),
                                  op=ALU.is_equal).then_inc(s_rowhot, 1)
            dve.wait_ge(s_tab, 1)
            step(dve.scalar_tensor_tensor(out=free_id[:], in0=table_ps[:, 0:NSC], scalar=0.0, in1=spare[:, 0:NSC],
                                          op0=ALU.is_equal, op1=ALU.mult), s_dec)
            dve.scalar_tensor_tensor(out=idx_all[:, 0:NSC], in0=free_id[:], scalar=-1.0, in1=table_ps[:, 0:NSC],
                                     op0=ALU.add, op1=ALU.add).then_inc(s_idx, 1)
            dve.tensor_scalar(idx_all[:, NSC:NSC + Q], spare[:, NSC:NSC + Q], -1.0, None, ALU.add).then_inc(s_idx, 1)

            n = blocks_of(dve)

            def weights_lo(b, k):
                dve.wait_ge(s_whi, b * NQ + k + 1)
                dve.tensor_tensor(out=w_lo[k][:], in0=raw[k][:], in1=w_hi[k][:].bitcast(f32),
                                  op=ALU.subtract).then_inc(s_wlo, 1)

            def z_lo_of(b):
                for c in range(DC):
                    dve.wait_ge(s_zhi, b * DC + c + 1)
                    dve.tensor_tensor(out=z_lo[:, c, :], in0=zt_ps[c][:, 0:TB], in1=z_hi[:, c, :].bitcast(f32),
                                      op=ALU.subtract).then_inc(s_zlo, 1)

            def take_weights(b, fresh):
                e = expert_of(dve, b)
                dve.wait_ge(s_get, (b + 1) * (16 * Q))
                if not fresh:
                    dve.wait_ge(s_rcur, b)
                dve.tensor_copy(r_next[:], z_row[:, :, ds(e + D, 1)].rearrange("p q a -> p (q a)")).then_inc(s_rnext, 1)

            def y_of(b):
                dve.wait_ge(s_h2, (b + 1) * HC)
                dve.wait_ge(s_b2r, (b + 1) * Q)
                dve.wait_ge(s_put, (b + 1) * (16 * Q))
                for q in range(Q):
                    dve.scalar_tensor_tensor(out=y[:, q, :], in0=y_ps[q][:, 0:D], scalar=r_cur[:, q:q + 1],
                                             in1=b2_r[:, q, :], op0=ALU.mult, op1=ALU.add).then_inc(s_y, 1)

            def weights_of_block(b, fresh):
                dve.wait_ge(s_rnext, b + 1)
                if not fresh:
                    dve.wait_ge(s_y, b * Q)
                dve.tensor_copy(r_cur[:], r_next[:]).then_inc(s_rcur, 1)

            def block_of_dve(b, fresh):
                if not fresh:
                    y_of(b - 1)
                weights_of_block(b, fresh)
                for c in range(HC):
                    i = c % NHX
                    dve.wait_ge(s_relu, b * HC + c + 1)
                    if not (fresh and c < NHX):
                        dve.wait_ge(s_h2, b * HC + c + 1 - NHX)
                    dve.tensor_copy(h_hi[i][:], h[c % NHP][:]).then_inc(s_hhi, 1)
                    dve.wait_ge(s_hhi, b * HC + c + 1)
                    dve.tensor_tensor(out=h_lo[i][:], in0=h[c % NHP][:], in1=h_hi[i][:].bitcast(f32),
                                      op=ALU.subtract).then_inc(s_hlo, 1)
                    if c == 0:
                        weights_lo(b, 2)
                    if c == 2:
                        weights_lo(b, 3)
                    if c == 4:
                        weights_lo(b + 1, 0)
                    if c == 6:
                        weights_lo(b + 1, 1)
                        take_weights(b + 1, False)
                z_lo_of(b + 1)

            weights_lo(0, 0)
            weights_lo(0, 1)
            take_weights(0, True)
            z_lo_of(0)
            block_of_dve(0, True)
            with dve.Fori(1, n) as b:
                block_of_dve(b, False)
            y_of(last_of(dve))

        @block.tensor
        def _(pe):
            pe.wait_ge(s_ys, 3)
            for oc in range(DC):
                for c in range(DC):
                    ins = pe.matmul(d_ps[:, oc * B:(oc + 1) * B], w2_sb[:, c, oc * P:(oc + 1) * P], ys2[:, c, :],
                                    start=(c == 0), stop=(c == DC - 1))
            ins.then_inc(s_sum, 1)
            pe.wait_ge(s_d, 5)
            pe.wait_ge(s_const, N_CONST)
            for c in range(DC):
                ins = pe.transpose(dr_ps[0:B, c * P:(c + 1) * P], dT[:, c, :], ident[:])
            ins.then_inc(s_dr, 1)
            pe.wait_ge(s_d, 6)
            for ic in range(DC):
                for c in range(DC):
                    ins = pe.matmul(m_ps[ic][:, 0:B * E], wT_sb[:, c, ic * P:(ic + 1) * P],
                                    dwr[:, c, :, :].rearrange("p b e -> p (b e)"), start=(c == 0), stop=(c == DC - 1))
            ins.then_inc(s_m, 1)

            def project(u, b):
                pe.wait_ge(s_xlo, b + 1)
                pe.wait_ge(s_wm, b + 1)
                for j in range(ST):
                    t = slice(j * P, (j + 1) * P)
                    for c in range(DC):
                        zp = z_ps[u % 2][:, j, :]
                        pe.matmul(zp, x_hi[u % NX][:, c, t], w_m[u % 2][:, 0, c, :], start=(c == 0), stop=False)
                        pe.matmul(zp, x_hi[u % NX][:, c, t], w_m[u % 2][:, 1, c, :], start=False, stop=False)
                        ins = pe.matmul(zp, x_lo[u % NX][:, c, t], w_m[u % 2][:, 0, c, :], start=False,
                                        stop=(c == DC - 1))
                ins.then_inc(s_zps, 1)

            pe.wait_ge(s_w, 6 * DC)
            for u in range(U):
                if u >= 2:
                    pe.wait_ge(s_z, u - 1)
                project(u, u)
            with pe.Fori(1, NG) as i:
                for u in range(U):
                    pe.wait_ge(s_z, i * U + u - 1)
                    project(u, i * U + u)

            pe.wait_ge(s_chosen, NG)
            chosen_all = chosen[:].rearrange("p n e -> p (n e)")
            pe.matmul(rank_ps[:, 0:NT * E], before[:], chosen_all, start=True, stop=True).then_inc(s_rank, 1)
            pe.matmul(total_ps[:, 0:NT * E], ones_bf[:], chosen_all, start=True, stop=True).then_inc(s_rank, 1)
            pe.wait_ge(s_colof, 4)
            for g in range(NTG):
                ins = pe.matmul(col_ps[:, g:g + 1],
                                col_of[:, g * TG:(g + 1) * TG].rearrange("p t s e o -> p (t s e o)"),
                                ident_bf[:, 0:1], start=True, stop=True)
            ins.then_inc(s_colps, 1)
            pe.wait_ge(s_hot2, TOPK)
            for g in range(NTG):
                pe.wait_ge(s_rowhot, g + 1)
                for t in range(TG):
                    for k in range(TOPK):
                        ins = pe.matmul(part_ps[g // BG][t * JW:(t + 1) * JW, (g % BG) * P:(g % BG + 1) * P],
                                        hot[:, k, g * TG + t].rearrange("p s e o -> p (s e o)"),
                                        row_hot[g % HOT][:, t, k, :], start=(k == 0), stop=(k == TOPK - 1))
                ins.then_inc(s_part, 1)
            pe.wait_ge(s_colhot, NTG)
            for g in range(NTG):
                if g % BG == 0:
                    pe.wait_ge(s_psb, g // BG + 1)
                ins = pe.matmul(table_ps[:, 0:NSC], partial[:, g * P:(g + 1) * P], col_hot[:, g, :],
                                start=(g == 0), stop=(g == NTG - 1))
            ins.then_inc(s_tab, 1)

            n = blocks_of(pe)

            def transpose_z(b):
                pe.wait_ge(s_get, (b + 1) * (16 * Q))
                for c in range(DC):
                    for q in range(Q):
                        ins = pe.transpose(zt_ps[c][:, q * P:(q + 1) * P], z_row[:, q, c * P:(c + 1) * P], ident[:])
                ins.then_inc(s_zt, 1)

            def w1(part, c, dc):
                o = dc * CQ * P + (c % CQ) * P
                return part[c // CQ][:, o:o + P]

            def w2(part, c):
                o = W1Q + (c % CQ) * D
                return part[c // CQ][:, o:o + D]

            def first_product(b, c, fresh):
                if c % CQ == 0:
                    pe.wait_ge(s_wlo, b * NQ + c // CQ + 1)
                if c == 0:
                    pe.wait_ge(s_zlo, (b + 1) * DC)
                if not (fresh and c < NHP):
                    pe.wait_ge(s_relu, b * HC + c + 1 - NHP)
                hp = h_ps[c % NHP][:, 0:TB]
                for dc in range(DC):
                    pe.matmul(hp, w1(w_hi, c, dc), z_hi[:, dc, :], start=(dc == 0), stop=False)
                    pe.matmul(hp, w1(w_hi, c, dc), z_lo[:, dc, :], start=False, stop=False)
                    ins = pe.matmul(hp, w1(w_lo, c, dc), z_hi[:, dc, :], start=False, stop=(dc == DC - 1))
                ins.then_inc(s_h1, 1)

            def second_product(b, c, fresh):
                pe.wait_ge(s_hlo, b * HC + c + 1)
                if c == 0 and not fresh:
                    pe.wait_ge(s_y, b * Q)
                for q in range(Q):
                    hi = h_hi[c % NHX][:, q * P:(q + 1) * P]
                    lo = h_lo[c % NHX][:, q * P:(q + 1) * P]
                    yp = y_ps[q][:, 0:D]
                    pe.matmul(yp, hi, w2(w_hi, c), start=(c == 0), stop=False)
                    pe.matmul(yp, hi, w2(w_lo, c), start=False, stop=False)
                    ins = pe.matmul(yp, lo, w2(w_hi, c), start=False, stop=(c == HC - 1))
                ins.then_inc(s_h2, 1)

            def block_of_pe(b, fresh):
                for c in range(HC):
                    if c == HC - 1:
                        transpose_z(b + 1)
                    first_product(b, c, fresh)
                    if c >= LAG:
                        second_product(b, c - LAG, fresh)
                for c in range(HC - LAG, HC):
                    second_product(b, c, fresh)

            transpose_z(0)
            block_of_pe(0, True)
            with pe.Fori(1, n) as b:
                block_of_pe(b, False)


def kernel(**inputs):
    import numpy as _np
    import concourse.bacc as _bacc
    from concourse import mybir as _mybir
    from concourse.bass_utils import run_bass_kernel_spmd as _run

    P = 128
    Q = 3
    a = {k: _np.asarray(v) for k, v in inputs.items()}
    x = a["x"]
    B, S, D = x.shape
    w = a["L0_cond_weight"]
    W1, W2 = a["L0_ffn_W1"], a["L0_ffn_W2"]
    E, _, H = W1.shape
    HC, DC, NQ = H // P, D // P, 4
    q1 = W1.reshape(E, DC, P, NQ, H // NQ).transpose(0, 3, 2, 1, 4).reshape(E, NQ, P, -1)
    q2 = W2.reshape(E, NQ, HC // NQ, P, D).transpose(0, 1, 3, 2, 4).reshape(E, NQ, P, -1)
    arrays = {
        "x": x.reshape(B * S, D),
        "xT": x.reshape(B * S, DC, P).transpose(2, 1, 0),
        "condT": a["cond_1024"].reshape(B, DC, P).transpose(2, 1, 0),
        "w": w,
        "wT": w.T,
        "wr": a["L0_ffn_Wr"],
        "br": a["L0_ffn_br"],
        "experts": _np.concatenate([q1, q2], axis=3),
        "b1": a["L0_ffn_b1"].reshape(E, HC, P).transpose(2, 0, 1),
        "b2": a["L0_ffn_b2"],
    }
    NT = B * S // P
    JW = 4 * E
    j, g = _np.arange(P)[:, None], _np.arange(NT * JW // P)[None, :]
    tile = g * (P // JW) + j // JW
    arrays["slot_weight"] = _np.where(j // (2 * E) % 2 == 0, P * tile, 1).astype(_np.float32)
    arrays = {f"in_{k}": _np.ascontiguousarray(v) for k, v in arrays.items()}
    nc = _bacc.Bacc("TRN2", target_bir_lowering=False, num_devices=1)
    args = [nc.dram_tensor(k, v.shape, _mybir.dt.from_np(v.dtype), kind="ExternalInput").ap()
            for k, v in arrays.items()]
    out = nc.dram_tensor("out", (B * S + Q * P, D), _mybir.dt.from_np(x.dtype), kind="ExternalOutput").ap()
    bass_adaln_moe_ffn(nc, *args, out)
    r = _run(nc, [arrays], core_ids=[0])
    return r.results[0]["out"][:B * S].reshape(B, S, D)
```

```python
import concourse.bass as bass
from concourse import mybir
from contextlib import ExitStack


def bass_adaln_moe_ffn(
    nc: bass.Bass,
    x: bass.AP,
    xT: bass.AP,
    condT: bass.AP,
    w: bass.AP,
    wT: bass.AP,
    wr: bass.AP,
    br: bass.AP,
    experts: bass.AP,
    b1: bass.AP,
    b2: bass.AP,
    slot_weight: bass.AP,
    out: bass.AP,
):
    f32 = mybir.dt.float32
    f32r = mybir.dt.float32r
    bf16 = mybir.dt.bfloat16
    i32 = mybir.dt.int32
    ALU = mybir.AluOpType
    ACT = mybir.ActivationFunctionType
    AX = mybir.AxisListType
    ds = bass.ds

    P = 128
    T, D = x.shape
    DC = D // P
    B = condT.shape[2]
    S = T // B
    ST = S // P
    NT = T // P
    E = br.shape[0]
    HC = b1.shape[2]
    NQ = experts.shape[1]
    CQ = HC // NQ
    QW = experts.shape[3]
    W1Q = DC * CQ * P
    TOPK = 2
    Q = (out.shape[0] - T) // P
    TB = Q * P
    MAXB = (TOPK * T + E * (TB - 1)) // TB
    NSC = MAXB * Q
    NJ = -(-T // TB)
    ZW = D + E
    EPS = 1e-8
    LAG = 2
    NHP = 3
    NHX = 4
    U = 8
    XG = 2
    NS = 4
    NX = 4
    GT = U * ST
    NG = NT // GT
    N_BEST = 10
    N_NEXT = 12
    JW = 2 * E * 2
    TG = P // JW
    NTG = NT // TG
    HOT = 4
    AHOT = 3
    ACT_GROUPS = (0, 6, 10, 14)
    DVE_GROUPS = tuple(g for g in range(NTG) if g not in ACT_GROUPS)
    POOL_COLS = 12
    INIT = 8

    z_rows = nc.dram_tensor("z_rows", (T + TB, ZW), f32, kind="Internal").ap()
    d_rows = nc.dram_tensor("d_rows", (B, ZW), f32, kind="Internal").ap()

    ctx = ExitStack()
    with ctx:
        def sb(name, shape, dt, stack=ctx):
            return stack.enter_context(nc.sbuf_tensor(name, shape, dt))

        def sem(name):
            return ctx.enter_context(nc.semaphore(name))

        idx_all = sb("idx_all", [P, NSC + Q], i32)
        block_expert = sb("block_expert", [P, MAXB + 1], i32)
        blocks_to = sb("blocks_to", [P, E], i32)
        idx_get = sb("idx_get", [P, Q], i32)
        idx_put = sb("idx_put", [P, Q], i32)
        n_blocks = sb("n_blocks", [P, 2], i32)
        b1_all = sb("b1_all", [P, E, HC], f32)
        b2_all = sb("b2_all", [P, E, D], f32)
        ident = sb("ident", [P, P], f32)
        zero = sb("zero", [P, ZW], f32)
        start = ExitStack()
        w_sb = sb("w_sb", [P, DC, D], f32, start)
        wT_sb = sb("wT_sb", [P, DC, D], f32, start)
        w2_sb = sb("w2_sb", [P, DC, D], f32, start)
        dwr = sb("dwr", [P, DC, B, E], f32, start)
        start.close()
        raw = [sb(f"raw{k}", [P, QW], f32) for k in range(NQ)]

        cond_sb = sb("cond_sb", [P, DC, B], f32)
        ys = sb("ys", [P, DC, B], f32)
        ys2 = sb("ys2", [P, DC, B], f32)
        wr_sb = sb("wr_sb", [P, DC, E], f32)
        v = sb("v", [P, DC, B], f32)
        root = sb("root", [P, DC, B], f32)
        exp_tables = sb("exp_tables", [P, 1], f32)
        rough = sb("rough", [P, DC, B], f32)
        fix = sb("fix", [P, DC, B], f32)
        dT = sb("dT", [P, DC, B], f32)
        m_all = sb("m_all", [P, 2, DC, B * E], f32r)
        d_sb = sb("d_sb", [B, ZW], f32)

        br_rep = sb("br_rep", [P, E], f32)
        logit = sb("logit", [P, GT, E], f32)
        tie = sb("tie", [P, GT, E], f32)
        top = sb("top", [P, GT], f32)
        inv = sb("inv", [P, GT], f32)
        best = sb("best", [P, GT], f32)
        rest = sb("rest", [P, GT, E], f32)
        tie2 = sb("tie2", [P, GT, E], f32)
        top2 = sb("top2", [P, GT], f32)
        inv2 = sb("inv2", [P, GT], f32)
        both = sb("both", [P, GT, E], f32)
        expo = sb("expo", [P, GT, E], f32)
        prob = sb("prob", [P, GT, E], f32)
        first = sb("first", [P, NT, E], f32)
        second = sb("second", [P, NT, E], f32)
        kept = sb("kept", [P, GT, E], f32)
        prefer = sb("prefer", [P, E], f32)
        chosen = sb("chosen", [P, E, NT], bf16)
        before = sb("before", [P, P], bf16)
        ones_bf = sb("ones_bf", [P, P], bf16)
        ident_bf = sb("ident_bf", [P, P], bf16)
        ones = sb("ones", [P, E * NT], f32)
        count_e = sb("count_e", [P, E], f32)
        nb_e = sb("nb_e", [P, E], f32)
        nb_end = sb("nb_end", [P, E], f32)
        began = sb("began", [P, NQ], f32)
        col_e = sb("col_e", [P, E], f32)
        steps = sb("steps", [P, NJ], f32)
        more = sb("more", [P, E, NJ], f32)
        blocks = sb("blocks", [P, MAXB + 1], f32)
        past = sb("past", [P, MAXB + 1, E], f32)
        ended = sb("ended", [P, MAXB + 1], f32)
        place = sb("place", [P, TOPK, NT], f32)
        over = sb("over", [P, TOPK, NT], f32)
        row = sb("row", [P, TOPK, NT], bf16)
        row_no = sb("row_no", [P, 1], f32)
        iota_row = sb("iota_row", [P, P], bf16)
        iota_col = sb("iota_col", [P, NSC], f32)
        weight_j = sb("weight_j", [P, NTG], f32)
        col_j = sb("col_j", [P, NTG], f32)
        spare = sb("spare", [P, NSC + Q], f32)
        free_id = sb("free_id", [P, NSC], f32)
        z_all = sb("z_all", [P, NT, ZW], f32)

        stage_a = ExitStack()
        d_rep = sb("d_rep", [P, B, ZW], f32, stage_a)
        x_buf = sb("x_buf", [P, U // XG, DC, XG * S], f32, stage_a)
        x_s = [sb(f"x_s{u}", [P, DC, S], f32, stage_a) for u in range(NS)]
        x_hi = [sb(f"x_hi{u}", [P, DC, S], f32r, stage_a) for u in range(NX)]
        x_lo = [sb(f"x_lo{u}", [P, DC, S], f32r, stage_a) for u in range(NX)]
        w_m = [sb(f"w_m{u}", [P, 2, DC, ZW], f32r, stage_a) for u in range(2)]
        stage_a.close()
        stage_b = ExitStack()
        w_hi = [sb(f"w_hi{k}", [P, QW], f32r, stage_b) for k in range(NQ)]
        w_lo = [sb(f"w_lo{k}", [P, QW], f32r, stage_b) for k in range(NQ)]
        stage_r = ExitStack()
        seen = sb("seen", [P, E * NT + 1], f32, stage_r)
        columns = sb("columns", [P, E * NT], f32, stage_r)
        seen_i = sb("seen_i", [P, E * NT], i32, stage_r)
        col_i = sb("col_i", [P, E * NT], i32, stage_r)
        rest_i = sb("rest_i", [P, E * NT], i32, stage_r)
        rank = sb("rank", [P, NT, E], f32, stage_r)
        mine = [sb(f"mine{k}", [P, NT, E], f32, stage_r) for k in range(TOPK)]
        hot = sb("hot", [P, TOPK, NT, 2, E, 2], bf16, stage_r)
        col_of = sb("col_of", [P, NT, 2, E, 2], bf16, stage_r)
        row_hot = [sb(f"row_hot{g}", [P, TG, TOPK, P], bf16, stage_r) for g in range(HOT)]
        row_hot2 = [sb(f"row_hot2_{g}", [P, TG, TOPK, P], bf16, stage_r) for g in range(AHOT)]
        away = [sb(f"away{i}", [P, TG, TOPK, P], bf16, stage_r) for i in range(2)]
        neg_row = sb("neg_row", [P, TOPK, NT], f32, stage_r)
        col_hot = sb("col_hot", [P, NTG, NSC], bf16, stage_r)
        partial = sb("partial", [P, NTG * P], bf16, stage_r)
        stage_r.close()
        h = [sb(f"h{i}", [P, TB], f32, stage_b) for i in range(NHP)]
        h_hi = [sb(f"h_hi{i}", [P, TB], f32r, stage_b) for i in range(NHX)]
        h_lo = [sb(f"h_lo{i}", [P, TB], f32r, stage_b) for i in range(NHX)]
        z_row = sb("z_row", [P, Q, ZW], f32, stage_b)
        z_hi = sb("z_hi", [P, DC, TB], f32r, stage_b)
        z_lo = sb("z_lo", [P, DC, TB], f32r, stage_b)
        y = sb("y", [P, Q, D], f32, stage_b)
        b2_r = sb("b2_r", [P, Q, D], f32, stage_b)
        r_next = sb("r_next", [P, Q], f32, stage_b)
        r_cur = sb("r_cur", [P, Q], f32, stage_b)
        stage_b.close()

        psum = ctx.enter_context(nc.psum_tensor("psum", [P, 8, 512], f32))
        bank = [psum[:, i, :] for i in range(8)]
        d_ps, dr_ps = bank[0], bank[1]
        m_ps = [bank[2 + c] for c in range(DC)]
        NZ = 8 // ST
        z_ps = [psum[:, (4 + ST * u) % 8:(4 + ST * u) % 8 + ST, 0:ZW] for u in range(NZ)]
        rank_ps, total_ps, table_ps, col_ps = bank[0], bank[1], bank[2], bank[3]
        BG = 512 // P
        part_ps = [bank[4 + i] for i in range(NTG // BG)]
        h_ps = [bank[i] for i in range(NHP)]
        y_ps = [bank[NHP + q] for q in range(Q)]
        zt_ps = [bank[NHP + Q + c] for c in range(DC)]

        s_in = sem("s_in")
        s_bias = sem("s_bias")
        s_const = sem("s_const")
        s_ys = sem("s_ys")
        s_sum = sem("s_sum")
        s_v = sem("s_v")
        s_root = sem("s_root")
        s_tables = sem("s_tables")
        s_d = sem("s_d")
        s_dr = sem("s_dr")
        s_m = sem("s_m")
        s_drow = sem("s_drow")
        s_dst = sem("s_dst")
        s_drep = [sem(f"s_drep{g}") for g in range(NG)]
        s_w = sem("s_w")
        s_x = [sem(f"s_x{g}") for g in range(U // XG)]
        s_xs = sem("s_xs")
        s_xhi = sem("s_xhi")
        s_xlo = sem("s_xlo")
        s_wm = sem("s_wm")
        s_zps = sem("s_zps")
        s_z = sem("s_z")
        s_best = sem("s_best")
        s_next = sem("s_next")
        s_exp = sem("s_exp")
        s_chosen = sem("s_chosen")
        s_zst = sem("s_zst")
        s_init = sem("s_init")
        s_rank = sem("s_rank")
        s_place = sem("s_place")
        s_block = sem("s_block")
        s_col = sem("s_col")
        s_colof = sem("s_colof")
        s_colps = sem("s_colps")
        s_colj = sem("s_colj")
        s_colhot = sem("s_colhot")
        s_hot = sem("s_hot")
        s_hot2 = sem("s_hot2")
        s_colhot2 = sem("s_colhot2")
        s_negrow = sem("s_negrow")
        s_away = sem("s_away")
        s_rowhot = sem("s_rowhot")
        s_rowhot2 = sem("s_rowhot2")
        s_part = sem("s_part")
        s_psb = sem("s_psb")
        s_tab = sem("s_tab")
        s_dec = sem("s_dec")
        s_blocks = sem("s_blocks")
        s_idx = sem("s_idx")
        s_raw = [sem(f"s_raw{k}") for k in range(NQ)]
        s_whi = sem("s_whi")
        s_wlo = sem("s_wlo")
        s_idxg0 = sem("s_idxg0")
        s_idxg = sem("s_idxg")
        s_idxp = sem("s_idxp")
        s_get = sem("s_get")
        s_put = sem("s_put")
        s_zt = sem("s_zt")
        s_zhi = sem("s_zhi")
        s_zlo = sem("s_zlo")
        s_rnext = sem("s_rnext")
        s_rcur = sem("s_rcur")
        s_b2r = sem("s_b2r")
        s_h1 = sem("s_h1")
        s_relu = sem("s_relu")
        s_hhi = sem("s_hhi")
        s_hlo = sem("s_hlo")
        s_h2 = sem("s_h2")
        s_y = sem("s_y")

        N_CONST = 17
        N_INPUTS = 4
        N_BIAS = 4
        N_BLOCKS = 4

        def back(c):
            return NHP if c >= NHP else c + 1 + (HC - 1 - c) % NHP

        def blocks_of(eng):
            eng.wait_ge(s_blocks, N_BLOCKS)
            return eng.value_load(n_blocks[0:1, 0:1], min_val=2, max_val=MAXB)

        def last_of(eng):
            return eng.value_load(n_blocks[0:1, 1:2], min_val=1, max_val=MAXB - 1)

        def expert_of(eng, b):
            return eng.value_load(block_expert[0:1, ds(b, 1)], min_val=0, max_val=E - 1)

        block = ctx.enter_context(nc.Block())

        @block.sync
        def _(sp):
            sp.dma_start(cond_sb[:], condT).then_inc(s_in, 16)
            sp.dma_start(w_sb[:], w.rearrange("(c p) o -> p c o", p=P)).then_inc(s_in, 16)
            sp.dma_start(wT_sb[:], wT.rearrange("(c p) i -> p c i", p=P)).then_inc(s_in, 16)
            sp.dma_start(wr_sb[:], wr.rearrange("(c p) e -> p c e", p=P)).then_inc(s_in, 16)
            for g in range(U // XG):
                sp.dma_start(x_buf[:, g], xT[:, :, g * XG * S:(g + 1) * XG * S]).then_inc(s_x[g], 16)

            def copy_x(i):
                rows = T // INIT
                sp.dma_start(out[ds(i * rows, rows), :], x[ds(i * rows, rows), :]).then_inc(s_init, 16)

            def store_z(g):
                sp.wait_ge(s_next, (g + 1) * N_NEXT)
                sp.dma_start(z_rows[ds(g * GT * P, GT * P), :].rearrange("(n p) z -> p n z", p=P),
                             z_all[:, ds(g * GT, GT), :]).then_inc(s_zst, 16)

            def load_weights(e, k):
                sp.dma_start(raw[k][:], experts[e, k]).then_inc(s_raw[k], 16)

            def load_x(i):
                for g in range(U // XG):
                    sp.wait_ge(s_xs, ((i - 1) * U + (g + 1) * XG) * DC)
                    sp.dma_start(x_buf[:, g], xT[:, :, ds((i * U + g * XG) * S, XG * S)]).then_inc(s_x[g], 16)

            copy_x(0)
            sp.dma_start(br_rep[:], br.rearrange("(a e) -> a e", a=1).to_broadcast([P, E])).then_inc(s_bias, 16)
            sp.dma_start(weight_j[:], slot_weight).then_inc(s_bias, 16)
            sp.wait_ge(s_drow, 2)
            sp.dma_start(d_rows, d_sb[:]).then_inc(s_dst, 16)
            sp.wait_ge(s_dst, 16)

            def load_d(g):
                sp.dma_start(d_rep[:, g * U:(g + 1) * U, :].rearrange("p b z -> p (b z)"),
                             d_rows[g * U:(g + 1) * U, :].rearrange("(a b) z -> a (b z)", a=1)
                             .to_broadcast([P, U * ZW])).then_inc(s_drep[g], 16)

            for g in range(2):
                load_d(g)
            load_x(1)
            for g in range(2, NG):
                load_d(g)
            with sp.Fori(2, NG) as i:
                load_x(i)
            for g in range(NG - 2):
                store_z(g)
            sp.dma_start(b1_all[:], b1).then_inc(s_bias, 16)
            sp.dma_start(b2_all[:].rearrange("p e d -> p (e d)"),
                         b2.rearrange("(a e) d -> a (e d)", a=1).to_broadcast([P, E * D])).then_inc(s_bias, 16)
            for k in range(NQ):
                load_weights(0, k)
            for i in range(1, 4):
                copy_x(i)
            sp.wait_ge(s_const, N_CONST)
            for q in range(Q):
                sp.dma_start(z_rows[T + q * P:T + (q + 1) * P, :], zero[:]).then_inc(s_zst, 16)
            for g in range(NG - 2, NG):
                store_z(g)
            sp.wait_ge(s_get, 16 * Q)
            for i in range(4, INIT):
                copy_x(i)
            sp.wait_ge(s_blocks, N_BLOCKS)
            for e in range(1, E):
                b = sp.value_load(blocks_to[0:1, e - 1:e], min_val=0, max_val=MAXB)
                for k in range(NQ):
                    sp.wait_ge(s_raw[k], e * 16)
                    sp.wait_ge(s_wlo, b * NQ + k + 1)
                    load_weights(e, k)
            sp.wait_ge(s_init, INIT * 16)

        @block.gpsimd
        def _(pool):
            exact = dict(allow_small_or_imprecise_dtypes=True)
            pool.memset(ident[:], 0.0).then_inc(s_const, 1)
            pool.memset(before[:], 0.0).then_inc(s_const, 1)
            pool.memset(ones_bf[:], 1.0).then_inc(s_const, 1)
            pool.memset(ones[:], 1.0).then_inc(s_const, 1)
            pool.memset(zero[:], 0.0).then_inc(s_const, 1)
            pool.memset(ident_bf[:], 0.0).then_inc(s_const, 1)
            pool.memset(d_sb[:], 1.0).then_inc(s_const, 1)
            pool.wait_ge(s_const, 7)
            pool.affine_select(out=ident[:], in_=ident[:], compare_op=ALU.not_equal, fill=1.0, base=0,
                               pattern=[[-1, P]], channel_multiplier=1).then_inc(s_const, 1)
            pool.affine_select(out=ident_bf[:], in_=ident_bf[:], compare_op=ALU.not_equal, fill=1.0, base=0,
                               pattern=[[-1, P]], channel_multiplier=1).then_inc(s_const, 1)
            pool.affine_select(out=before[:], in_=before[:], compare_op=ALU.is_ge, fill=1.0, base=0,
                               pattern=[[-1, P]], channel_multiplier=1).then_inc(s_const, 1)
            pool.iota(prefer[:], pattern=[[-1, E]], base=E, channel_multiplier=0, **exact).then_inc(s_const, 1)
            pool.iota(steps[:], pattern=[[TB, NJ]], base=0, channel_multiplier=0, **exact).then_inc(s_const, 1)
            pool.iota(blocks[:], pattern=[[1, MAXB + 1]], base=0, channel_multiplier=0, **exact).then_inc(s_const, 1)
            pool.iota(iota_row[:], pattern=[[1, P]], base=0, channel_multiplier=0, **exact).then_inc(s_const, 1)
            pool.iota(iota_col[:], pattern=[[1, NSC]], base=0, channel_multiplier=0, **exact).then_inc(s_const, 1)
            pool.iota(row_no[:], pattern=[[0, 1]], base=1, channel_multiplier=1, **exact).then_inc(s_const, 1)
            pool.iota(spare[:].rearrange("p (b q) -> p b q", q=Q), pattern=[[0, MAXB + 1], [P, Q]],
                      base=T + 1, channel_multiplier=1, **exact).then_inc(s_const, 1)

            pool.wait_ge(s_const, N_CONST)
            for q in range(Q):
                pool.dma_start(out[T + q * P:T + (q + 1) * P, :], zero[:, 0:D]).then_inc(s_put, 16)

            def x_lo_of(u, b):
                pool.wait_ge(s_xhi, b + 1)
                pool.tensor_tensor(out=x_lo[u % NX][:], in0=x_s[u % NS][:], in1=x_hi[u % NX][:].bitcast(f32),
                                   op=ALU.subtract).then_inc(s_xlo, 1)

            def router_columns(u, b, fresh):
                if not fresh:
                    pool.wait_ge(s_zps, b - 1)
                pool.tensor_copy(w_m[u % 2][:, :, :, D:ZW], m_all[:, :, :, ds(b * E, E)]).then_inc(s_wm, 1)

            for u in range(U):
                x_lo_of(u, u)
                if u == 0:
                    pool.wait_ge(s_w, 6 * DC)
                router_columns(u, u, u < 2)
            with pool.Fori(1, NG) as i:
                for u in range(U):
                    x_lo_of(u, i * U + u)
                    router_columns(u, i * U + u, False)

            pool.wait_ge(s_colj, 1)
            for g in range(POOL_COLS):
                pool.tensor_scalar(col_hot[:, g, :], iota_col[:], col_j[:, g:g + 1], weight_j[:, g:g + 1],
                                   ALU.is_equal, ALU.mult).then_inc(s_colhot, 1)

            n = blocks_of(pool)
            pool.wait_ge(s_idx, 2)

            def gather(b, copied, count, constant):
                pool.tensor_copy(idx_get[:], idx_all[:, ds(b * Q, Q)]).then_inc(copied, 1)
                pool.wait_ge(*constant)
                pool.wait_ge(copied, count)
                for q in range(Q):
                    pool.indirect_dma_start(
                        out=z_row[:, q, :], out_offset=None, in_=z_rows,
                        in_offset=bass.IndirectOffsetOnAxis(ap=idx_get[:, q:q + 1], axis=0)).then_inc(s_get, 16)

            def row_free(b):
                pool.wait_ge(s_zt, b + 1)
                pool.wait_ge(s_rnext, b + 1)

            def scatter_add(b):
                pool.tensor_copy(idx_put[:], idx_all[:, ds(b * Q, Q)]).then_inc(s_idxp, 1)
                pool.wait_ge(s_init, INIT * 16)
                pool.wait_ge(s_idxp, b + 1)
                for q in range(Q):
                    pool.indirect_dma_start(
                        out=out, out_offset=bass.IndirectOffsetOnAxis(ap=idx_put[:, q:q + 1], axis=0),
                        in_=y[:, q, :], in_offset=None, compute_op=ALU.add).then_inc(s_put, 16)

            rows_stored = (s_zst, (NG + Q) * 16)
            gather(0, s_idxg0, 1, rows_stored)
            row_free(0)
            gather(1, s_idxg0, 2, rows_stored)
            with pool.Fori(1, n) as b:
                row_free(b)
                gather(b + 1, s_idxg, b, (s_next, NG * N_NEXT))
                pool.wait_ge(s_y, b * Q)
                pool.wait_ge(s_put, b * (16 * Q))
                scatter_add(b - 1)
            last = last_of(pool)
            pool.wait_ge(s_y, (last + 1) * Q)
            pool.wait_ge(s_put, (last + 1) * (16 * Q))
            scatter_add(last)
            for k in range(NQ):
                pool.wait_ge(s_raw[k], E * 16)
            pool.wait_ge(s_put, (last + 2) * (16 * Q))

        @block.scalar
        def _(act):
            act.wait_ge(s_v, 1)
            act.activation(root[:], v[:], ACT.Sqrt).then_inc(s_root, 1)
            act.activation(exp_tables[:], v[:, 0, 0:1], ACT.Exp).then_inc(s_tables, 1)

            def x_s_of(u, i, b):
                if u % XG == 0:
                    act.wait_ge(s_x[u // XG], (i + 1) * 16)
                for c in range(DC):
                    act.activation(x_s[u % NS][:, c, :], x_buf[:, u // XG, c, (u % XG) * S:(u % XG + 1) * S],
                                   ACT.Copy, scale=ys[:, c, ds(b, 1)]).then_inc(s_xs, 1)

            def x_hi_of(u, b):
                act.wait_ge(s_xs, (b + 1) * DC)
                act.activation(x_hi[u % NX][:], x_s[u % NS][:], ACT.Copy).then_inc(s_xhi, 1)

            def softmax_exp(g):
                act.wait_ge(s_best, g * N_BEST + 3)
                act.activation(expo[:], logit[:], ACT.Exp).then_inc(s_exp, 1)

            act.wait_ge(s_ys, 1)
            for u in range(U):
                if u >= NS:
                    act.wait_ge(s_xlo, u - NS + 1)
                x_s_of(u, 0, u)
                if u > NX:
                    act.wait_ge(s_zps, u - NX)
                if u >= 1:
                    x_hi_of(u - 1, u - 1)
            with act.Fori(1, NG) as i:
                for u in range(U):
                    act.wait_ge(s_xlo, i * U + u - NS + 1)
                    x_s_of(u, i, i * U + u)
                    act.wait_ge(s_zps, i * U + u - NX)
                    x_hi_of((u - 1) % U, i * U + u - 1)
                    if u == 6:
                        softmax_exp(i - 1)
            act.wait_ge(s_zps, NG * U - NX)
            x_hi_of(U - 1, NG * U - 1)
            softmax_exp(NG - 1)

            def row_hot_of(n, g):
                if n >= AHOT:
                    act.wait_ge(s_part, ACT_GROUPS[n - AHOT] + 1)
                for t in range(TG):
                    for k in range(TOPK):
                        act.activation(away[n % 2][:, t, k, :], iota_row[:], ACT.Abs,
                                       bias=neg_row[:, k, g * TG + t:g * TG + t + 1]).then_inc(s_away, 1)
                act.wait_ge(s_away, (n + 1) * TG * TOPK)
                act.activation(row_hot2[n % AHOT][:], away[n % 2][:], ACT.Relu, bias=ones[:, 0:1],
                               scale=-1.0).then_inc(s_rowhot2, 1)

            def partial_of(i):
                act.wait_ge(s_part, (i + 1) * BG)
                act.activation(partial[:, i * 512:(i + 1) * 512], part_ps[i], ACT.Copy).then_inc(s_psb, 1)

            act.wait_ge(s_negrow, 1)
            for n, g in enumerate(ACT_GROUPS):
                row_hot_of(n, g)
                if n == 0:
                    for k in range(TOPK):
                        act.wait_ge(s_hot, TOPK + k + 1)
                        act.activation(hot[:, k, :, 1], hot[:, k, :, 0], ACT.Copy,
                                       scale=row_no[:, 0:1]).then_inc(s_hot2, 1)
                else:
                    partial_of(n - 1)
            for i in range(len(ACT_GROUPS) - 1, NTG // BG):
                partial_of(i)

            n = blocks_of(act)
            act.wait_ge(s_bias, N_BIAS * 16)

            def weights_hi(b, k, e, fresh):
                act.wait_ge(s_raw[k], e * 16 + 16)
                if not fresh:
                    act.wait_ge(s_h2, (b - 1) * HC + (k + 1) * CQ)
                act.activation(w_hi[k][:], raw[k][:], ACT.Copy).then_inc(s_whi, 1)

            def z_hi_of(b, fresh):
                act.wait_ge(s_zt, b + 1)
                if not fresh:
                    act.wait_ge(s_h1, b * HC)
                for c in range(DC):
                    act.activation(z_hi[:, c, :], zt_ps[c][:, 0:TB], ACT.Copy).then_inc(s_zhi, 1)

            def block_of_act(b, fresh):
                e = expert_of(act, b)
                e_next = expert_of(act, b + 1)
                for c in range(HC):
                    act.wait_ge(s_h1, b * HC + c + 1)
                    if not (fresh and c < NHP):
                        act.wait_ge(s_hlo, b * HC + c + 1 - back(c))
                    act.activation(h[c % NHP][:], h_ps[c % NHP][:, 0:TB], ACT.Relu,
                                   bias=b1_all[:, ds(e, 1), c]).then_inc(s_relu, 1)
                    if c == 0:
                        weights_hi(b, 2, e, fresh)
                    if c == 1:
                        act.wait_ge(s_rcur, b + 1)
                        for q in range(Q):
                            act.activation(b2_r[:, q, :], b2_all[:, ds(e, 1), :].rearrange("p a d -> p (a d)"),
                                           ACT.Copy, scale=r_cur[:, q:q + 1]).then_inc(s_b2r, 1)
                    if c == 2:
                        weights_hi(b, 3, e, fresh)
                    if c == 4:
                        weights_hi(b + 1, 0, e_next, False)
                    if c == 5:
                        weights_hi(b + 1, 1, e_next, False)
                z_hi_of(b + 1, False)

            e_first = expert_of(act, 0)
            weights_hi(0, 0, e_first, True)
            weights_hi(0, 1, e_first, True)
            z_hi_of(0, True)
            block_of_act(0, True)
            with act.Fori(1, n) as b:
                block_of_act(b, False)

        @block.vector
        def _(dve):
            done = {}

            def step(ins, s):
                done[s.name] = done.get(s.name, 0) + 1
                ins.then_inc(s, 1)
                dve.wait_ge(s, done[s.name])

            dve.wait_ge(s_in, N_INPUTS * 16)
            step(dve.tensor_scalar(ys[:], cond_sb[:], float(D) ** -0.5, None, ALU.mult), s_ys)
            dve.tensor_tensor(out=ys2[:], in0=ys[:], in1=ys[:], op=ALU.mult).then_inc(s_ys, 1)
            dve.tensor_tensor(out=w2_sb[:], in0=w_sb[:], in1=w_sb[:], op=ALU.mult).then_inc(s_ys, 1)
            for c in range(DC):
                for u in range(2):
                    dve.tensor_copy(w_m[u][:, 0, c, 0:D], w_sb[:, c, :]).then_inc(s_w, 1)
            dve.wait_ge(s_w, 2 * DC)
            for c in range(DC):
                for u in range(2):
                    dve.tensor_tensor(out=w_m[u][:, 1, c, 0:D], in0=w_sb[:, c, :],
                                      in1=w_m[u][:, 0, c, 0:D].bitcast(f32), op=ALU.subtract).then_inc(s_w, 1)
            dve.wait_ge(s_sum, 1)
            step(dve.tensor_scalar(v[:], d_ps[:, 0:DC * B].rearrange("p (c b) -> p c b", c=DC), EPS, None, ALU.add), s_v)
            dve.wait_ge(s_root, 1)
            step(dve.reciprocal(rough[:], root[:]), s_d)
            step(dve.tensor_tensor(out=fix[:], in0=rough[:], in1=rough[:], op=ALU.mult), s_d)
            step(dve.tensor_tensor(out=fix[:], in0=fix[:], in1=v[:], op=ALU.mult), s_d)
            step(dve.tensor_scalar(fix[:], fix[:], -0.5, 1.5, ALU.mult, ALU.add), s_d)
            step(dve.tensor_tensor(out=dT[:], in0=fix[:], in1=rough[:], op=ALU.mult), s_d)
            dve.tensor_tensor(out=dwr[:], in0=dT[:].unsqueeze(3).to_broadcast([P, DC, B, E]),
                              in1=wr_sb[:].unsqueeze(2).to_broadcast([P, DC, B, E]), op=ALU.mult).then_inc(s_d, 1)
            dve.wait_ge(s_dr, 1)
            dve.wait_ge(s_const, N_CONST)
            for c in range(DC):
                dve.tensor_copy(d_sb[:, c * P:(c + 1) * P], dr_ps[0:B, c * P:(c + 1) * P]).then_inc(s_drow, 1)
            dve.wait_ge(s_m, 1)
            for c in range(DC):
                dve.tensor_copy(m_all[:, 0, c, :], m_ps[c][:, 0:B * E]).then_inc(s_w, 1)
            dve.wait_ge(s_w, 5 * DC)
            for c in range(DC):
                dve.tensor_tensor(out=m_all[:, 1, c, :], in0=m_ps[c][:, 0:B * E],
                                  in1=m_all[:, 0, c, :].bitcast(f32), op=ALU.subtract).then_inc(s_w, 1)
            dve.wait_ge(s_w, 6 * DC)

            def z_of(u, b):
                dve.wait_ge(s_zps, b + 1)
                dve.tensor_tensor(out=z_all[:, ds(b * ST, ST), :], in0=z_ps[u % NZ],
                                  in1=d_rep[:, ds(b, 1), :].to_broadcast([P, ST, ZW]), op=ALU.mult).then_inc(s_z, 1)

            def over_e(a):
                return a[:].unsqueeze(2).to_broadcast([P, GT, E])

            prefer_g = prefer[:].unsqueeze(1).to_broadcast([P, GT, E])

            def best_step(n, g, has_next):
                if n == 1:
                    dve.wait_ge(s_z, (g + 1) * U)
                else:
                    dve.wait_ge(s_best, g * N_BEST + n - 1)
                if n == 1:
                    ins = dve.tensor_tensor(out=logit[:], in0=z_all[:, ds(g * GT, GT), D:ZW],
                                            in1=br_rep[:].unsqueeze(1).to_broadcast([P, GT, E]), op=ALU.add)
                if n == 2:
                    ins = dve.tensor_reduce(top[:], logit[:], AX.X, ALU.max)
                if n == 3:
                    ins = dve.tensor_tensor(out=logit[:], in0=logit[:], in1=over_e(top), op=ALU.subtract)
                if n == 4:
                    dve.wait_ge(s_exp, g + 1)
                    ins = dve.tensor_reduce(top[:], expo[:], AX.X, ALU.add)
                if n == 5:
                    ins = dve.reciprocal(inv[:], top[:])
                if n == 6:
                    if has_next:
                        dve.wait_ge(s_next, (g - 1) * N_NEXT + 9)
                    ins = dve.tensor_tensor(out=prob[:], in0=expo[:], in1=over_e(inv), op=ALU.mult)
                if n == 7:
                    ins = dve.tensor_reduce(top[:], prob[:], AX.X, ALU.max)
                if n == 8:
                    ins = dve.tensor_tensor(out=tie[:], in0=prob[:], in1=over_e(top), op=ALU.is_equal)
                if n == 9:
                    ins = dve.tensor_tensor(out=tie[:], in0=tie[:], in1=prefer_g, op=ALU.mult)
                if n == 10:
                    ins = dve.tensor_reduce(best[:], tie[:], AX.X, ALU.max)
                ins.then_inc(s_best, 1)

            def next_step(n, g):
                tiles = ds(g * GT, GT)
                first_g, second_g = first[:, tiles, :], second[:, tiles, :]
                if n == 1:
                    dve.wait_ge(s_best, (g + 1) * N_BEST)
                else:
                    dve.wait_ge(s_next, g * N_NEXT + n - 1)
                if n == 1:
                    ins = dve.tensor_tensor(out=first_g, in0=tie[:], in1=over_e(best), op=ALU.is_equal)
                if n == 2:
                    ins = dve.scalar_tensor_tensor(out=rest[:], in0=first_g, scalar=-4.0, in1=prob[:],
                                                   op0=ALU.mult, op1=ALU.add)
                if n == 3:
                    ins = dve.tensor_reduce(top2[:], rest[:], AX.X, ALU.max)
                if n == 4:
                    ins = dve.tensor_tensor(out=tie2[:], in0=rest[:], in1=over_e(top2), op=ALU.is_equal)
                if n == 5:
                    ins = dve.tensor_tensor(out=tie2[:], in0=tie2[:], in1=prefer_g, op=ALU.mult)
                if n == 6:
                    ins = dve.tensor_reduce(top2[:], tie2[:], AX.X, ALU.max)
                if n == 7:
                    ins = dve.tensor_tensor(out=second_g, in0=tie2[:], in1=over_e(top2), op=ALU.is_equal)
                if n == 8:
                    ins = dve.tensor_tensor(out=both[:], in0=first_g, in1=second_g, op=ALU.add)
                if n == 9:
                    dve.tensor_copy(chosen[:, :, tiles].rearrange("p e n -> p n e"), both[:]).then_inc(s_chosen, 1)
                    ins = dve.tensor_tensor(out=kept[:], in0=prob[:], in1=both[:], op=ALU.mult)
                if n == 10:
                    ins = dve.tensor_reduce(top2[:], kept[:], AX.X, ALU.add)
                if n == 11:
                    ins = dve.reciprocal(inv2[:], top2[:])
                if n == 12:
                    ins = dve.tensor_tensor(out=z_all[:, tiles, D:ZW], in0=kept[:], in1=over_e(inv2), op=ALU.mult)
                ins.then_inc(s_next, 1)

            BEST = ((1, 2), (3,), (), (), (4, 5), (6, 7), (8, 9), (10,))
            NEXT = ((1, 2), (3, 4), (5, 6), (7, 8), (9,), (10,), (11,), (12,))

            def route(u, g_best, g_next):
                for k in range(2):
                    if g_next is not None and k < len(NEXT[u]):
                        next_step(NEXT[u][k], g_next)
                    if k < len(BEST[u]):
                        best_step(BEST[u][k], g_best, g_next is not None)

            dve.wait_ge(s_drep[0], 16)
            for u in range(U):
                z_of(u, u)
            dve.wait_ge(s_bias, 2 * 16)
            dve.wait_ge(s_drep[1], 16)
            for u in range(U):
                z_of(u, U + u)
                route(u, 0, None)
            for g in range(2, NG):
                dve.wait_ge(s_drep[g], 16)
            with dve.Fori(2, NG) as i:
                for u in range(U):
                    z_of(u, i * U + u)
                    route(u, i - 1, i - 2)
            for u in range(U):
                route(u, NG - 1, NG - 2)
            for n in range(1, N_NEXT + 1):
                next_step(n, NG - 1)

            def e_major(a):
                return a[:, 0:E * NT].rearrange("p (e n) -> p e n", e=E)

            def by_tile(a):
                return a[:, 0:E * NT].rearrange("p (e n) -> p n e", e=E)

            dve.wait_ge(s_zps, NT // ST)
            step(dve.memset(seen[:, 0:1], 0.0), s_place)
            dve.wait_ge(s_rank, 2)
            step(dve.tensor_tensor_scan(seen[:, 1:E * NT + 1], ones[:], total_ps[:, 0:NT * E], 0.0, ALU.mult,
                                        ALU.add), s_place)
            start_e = e_major(seen)[:, :, 0]
            end_e = seen[:, 1:E * NT + 1].rearrange("p (e n) -> p e n", e=E)[:, :, NT - 1]

            def last(s):
                dve.wait_ge(s, done[s.name])

            def signal(ins, s):
                done[s.name] = done.get(s.name, 0) + 1
                ins.then_inc(s, 1)

            signal(dve.tensor_tensor(out=e_major(seen_i), in0=e_major(seen),
                                     in1=start_e.unsqueeze(2).to_broadcast([P, E, NT]), op=ALU.subtract), s_place)
            signal(dve.tensor_tensor(out=count_e[:], in0=end_e, in1=start_e, op=ALU.subtract), s_block)
            last(s_place)
            signal(dve.tensor_single_scalar(rest_i[:], seen_i[:], P - 1, op=ALU.bitwise_and), s_place)
            last(s_block)
            signal(dve.tensor_tensor(out=more[:], in0=count_e[:].unsqueeze(2).to_broadcast([P, E, NJ]),
                                     in1=steps[:].unsqueeze(1).to_broadcast([P, E, NJ]), op=ALU.is_gt), s_block)
            dve.tensor_single_scalar(col_i[:], seen_i[:], P.bit_length() - 1,
                                     op=ALU.logical_shift_right).then_inc(s_col, 1)
            last(s_block)
            signal(dve.tensor_reduce(nb_e[:], more[:], AX.X, ALU.add), s_block)
            last(s_place)
            signal(dve.tensor_tensor(out=rank[:], in0=by_tile(rank_ps), in1=by_tile(rest_i), op=ALU.add), s_place)
            last(s_block)
            signal(dve.tensor_tensor_scan(nb_end[:], ones[:, 0:E], nb_e[:], 0.0, ALU.mult, ALU.add), s_block)
            last(s_place)
            signal(dve.tensor_tensor(out=mine[0][:], in0=first[:], in1=rank[:], op=ALU.mult), s_place)
            last(s_block)
            signal(dve.tensor_tensor(out=past[:], in0=blocks[:].unsqueeze(2).to_broadcast([P, MAXB + 1, E]),
                                     in1=nb_end[:].unsqueeze(1).to_broadcast([P, MAXB + 1, E]), op=ALU.is_ge), s_block)
            dve.tensor_copy(blocks_to[:], nb_end[:]).then_inc(s_blocks, 1)
            dve.tensor_copy(n_blocks[:, 0:1], nb_end[:, E - 1:E]).then_inc(s_blocks, 1)
            dve.tensor_scalar(n_blocks[:, 1:2], nb_end[:, E - 1:E], -1.0, None, ALU.add).then_inc(s_blocks, 1)
            last(s_place)
            signal(dve.tensor_reduce(place[:, 0, :], mine[0][:], AX.X, ALU.add), s_place)
            last(s_block)
            signal(dve.tensor_reduce(ended[:], past[:], AX.X, ALU.add), s_block)
            signal(dve.tensor_tensor(out=col_e[:], in0=nb_end[:], in1=nb_e[:], op=ALU.subtract), s_block)
            signal(dve.tensor_tensor(out=mine[1][:], in0=second[:], in1=rank[:], op=ALU.mult), s_place)
            last(s_block)
            dve.tensor_scalar(block_expert[:], ended[:], float(E - 1), None, ALU.min).then_inc(s_blocks, 1)
            for k in range(NQ):
                dve.memset(began[:, k:k + 1], 0.0).then_inc(s_wlo, 1)
            dve.wait_ge(s_col, 1)
            signal(dve.scalar_tensor_tensor(out=e_major(columns), in0=col_e[:].unsqueeze(2).to_broadcast([P, E, NT]),
                                            scalar=float(Q), in1=e_major(col_i), op0=ALU.mult, op1=ALU.add), s_block)
            last(s_place)
            signal(dve.tensor_reduce(place[:, 1, :], mine[1][:], AX.X, ALU.add), s_place)
            last(s_block)
            for half in range(2):
                dve.tensor_copy(col_of[:, :, half, :, 0], by_tile(columns)).then_inc(s_colof, 1)
            last(s_place)
            signal(dve.tensor_scalar(over[:], place[:], float(P), None, ALU.is_ge), s_place)
            for half in range(2):
                dve.tensor_scalar(col_of[:, :, half, :, 1], by_tile(columns), 1.0, None, ALU.add).then_inc(s_colof, 1)
            last(s_place)
            dve.scalar_tensor_tensor(out=neg_row[:], in0=over[:], scalar=float(P), in1=place[:],
                                     op0=ALU.mult, op1=ALU.subtract).then_inc(s_negrow, 1)
            for k, is_mine in enumerate((first, second)):
                dve.tensor_tensor(out=hot[:, k, :, 0, :, 1], in0=is_mine[:],
                                  in1=over[:, k, :].unsqueeze(2).to_broadcast([P, NT, E]), op=ALU.mult).then_inc(s_hot, 1)
            signal(dve.scalar_tensor_tensor(out=row[:], in0=over[:], scalar=-float(P), in1=place[:],
                                            op0=ALU.mult, op1=ALU.add), s_place)
            for k, is_mine in enumerate((first, second)):
                dve.wait_ge(s_hot, k + 1)
                dve.tensor_tensor(out=hot[:, k, :, 0, :, 0], in0=is_mine[:], in1=hot[:, k, :, 0, :, 1],
                                  op=ALU.subtract).then_inc(s_hot, 1)
            last(s_place)

            for n, g in enumerate(DVE_GROUPS):
                if n >= HOT:
                    dve.wait_ge(s_part, DVE_GROUPS[n - HOT] + 1)
                dve.tensor_tensor(out=row_hot[n % HOT][:].rearrange("p t k r -> p k t r"),
                                  in0=iota_row[:].unsqueeze(1).unsqueeze(1).to_broadcast([P, TOPK, TG, P]),
                                  in1=row[:, :, g * TG:(g + 1) * TG].unsqueeze(3).to_broadcast([P, TOPK, TG, P]),
                                  op=ALU.is_equal).then_inc(s_rowhot, 1)
                if n == 0:
                    dve.wait_ge(s_colps, 1)
                    dve.tensor_copy(col_j[:], col_ps[:, 0:NTG]).then_inc(s_colj, 1)
            dve.wait_ge(s_colj, 1)
            for g in range(POOL_COLS, NTG):
                dve.tensor_scalar(col_hot[:, g, :], iota_col[:], col_j[:, g:g + 1], weight_j[:, g:g + 1],
                                  ALU.is_equal, ALU.mult).then_inc(s_colhot2, 1)
            dve.wait_ge(s_tab, 1)
            step(dve.scalar_tensor_tensor(out=free_id[:], in0=table_ps[:, 0:NSC], scalar=0.0, in1=spare[:, 0:NSC],
                                          op0=ALU.is_equal, op1=ALU.mult), s_dec)
            dve.scalar_tensor_tensor(out=idx_all[:, 0:NSC], in0=free_id[:], scalar=-1.0, in1=table_ps[:, 0:NSC],
                                     op0=ALU.add, op1=ALU.add).then_inc(s_idx, 1)
            dve.tensor_scalar(idx_all[:, NSC:NSC + Q], spare[:, NSC:NSC + Q], -1.0, None, ALU.add).then_inc(s_idx, 1)

            n = blocks_of(dve)

            def weights_lo(b, k):
                dve.wait_ge(s_whi, b * NQ + k + 1)
                dve.tensor_tensor(out=w_lo[k][:], in0=raw[k][:], in1=w_hi[k][:].bitcast(f32),
                                  op=ALU.subtract).then_inc(s_wlo, 1)

            def z_lo_of(b):
                for c in range(DC):
                    dve.wait_ge(s_zhi, b * DC + c + 1)
                    dve.tensor_tensor(out=z_lo[:, c, :], in0=zt_ps[c][:, 0:TB], in1=z_hi[:, c, :].bitcast(f32),
                                      op=ALU.subtract).then_inc(s_zlo, 1)

            def take_weights(b, fresh):
                e = expert_of(dve, b)
                dve.wait_ge(s_get, (b + 1) * (16 * Q))
                if not fresh:
                    dve.wait_ge(s_rcur, b)
                dve.tensor_copy(r_next[:], z_row[:, :, ds(e + D, 1)].rearrange("p q a -> p (q a)")).then_inc(s_rnext, 1)

            def y_of(b):
                dve.wait_ge(s_h2, (b + 1) * HC)
                dve.wait_ge(s_b2r, (b + 1) * Q)
                dve.wait_ge(s_put, (b + 1) * (16 * Q))
                for q in range(Q):
                    dve.scalar_tensor_tensor(out=y[:, q, :], in0=y_ps[q][:, 0:D], scalar=r_cur[:, q:q + 1],
                                             in1=b2_r[:, q, :], op0=ALU.mult, op1=ALU.add).then_inc(s_y, 1)

            def weights_of_block(b, fresh):
                dve.wait_ge(s_rnext, b + 1)
                if not fresh:
                    dve.wait_ge(s_y, b * Q)
                dve.tensor_copy(r_cur[:], r_next[:]).then_inc(s_rcur, 1)

            def block_of_dve(b, fresh):
                if not fresh:
                    y_of(b - 1)
                weights_of_block(b, fresh)
                for c in range(HC):
                    i = c % NHX
                    dve.wait_ge(s_relu, b * HC + c + 1)
                    if not (fresh and c < NHX):
                        dve.wait_ge(s_h2, b * HC + c + 1 - NHX)
                    dve.tensor_copy(h_hi[i][:], h[c % NHP][:]).then_inc(s_hhi, 1)
                    dve.wait_ge(s_hhi, b * HC + c + 1)
                    dve.tensor_tensor(out=h_lo[i][:], in0=h[c % NHP][:], in1=h_hi[i][:].bitcast(f32),
                                      op=ALU.subtract).then_inc(s_hlo, 1)
                    if c == 1:
                        weights_lo(b, 2)
                    if c == 3:
                        weights_lo(b, 3)
                    if c == (HC - 2 if fresh else 3):
                        take_weights(b + 1, False)
                    if c == 4:
                        weights_lo(b + 1, 0)
                    if c == 5:
                        weights_lo(b + 1, 1)
                z_lo_of(b + 1)

            weights_lo(0, 0)
            weights_lo(0, 1)
            take_weights(0, True)
            z_lo_of(0)
            block_of_dve(0, True)
            with dve.Fori(1, n) as b:
                block_of_dve(b, False)
            y_of(last_of(dve))

        @block.tensor
        def _(pe):
            pe.wait_ge(s_ys, 3)
            for oc in range(DC):
                for c in range(DC):
                    ins = pe.matmul(d_ps[:, oc * B:(oc + 1) * B], w2_sb[:, c, oc * P:(oc + 1) * P], ys2[:, c, :],
                                    start=(c == 0), stop=(c == DC - 1))
            ins.then_inc(s_sum, 1)
            pe.wait_ge(s_d, 5)
            pe.wait_ge(s_const, N_CONST)
            for c in range(DC):
                ins = pe.transpose(dr_ps[0:B, c * P:(c + 1) * P], dT[:, c, :], ident[:])
            ins.then_inc(s_dr, 1)
            pe.wait_ge(s_d, 6)
            for ic in range(DC):
                for c in range(DC):
                    ins = pe.matmul(m_ps[ic][:, 0:B * E], wT_sb[:, c, ic * P:(ic + 1) * P],
                                    dwr[:, c, :, :].rearrange("p b e -> p (b e)"), start=(c == 0), stop=(c == DC - 1))
            ins.then_inc(s_m, 1)

            def project(u, b):
                pe.wait_ge(s_xlo, b + 1)
                pe.wait_ge(s_wm, b + 1)
                for j in range(ST):
                    t = slice(j * P, (j + 1) * P)
                    for c in range(DC):
                        zp = z_ps[u % NZ][:, j, :]
                        pe.matmul(zp, x_hi[u % NX][:, c, t], w_m[u % 2][:, 0, c, :], start=(c == 0), stop=False)
                        pe.matmul(zp, x_hi[u % NX][:, c, t], w_m[u % 2][:, 1, c, :], start=False, stop=False)
                        ins = pe.matmul(zp, x_lo[u % NX][:, c, t], w_m[u % 2][:, 0, c, :], start=False,
                                        stop=(c == DC - 1))
                ins.then_inc(s_zps, 1)

            pe.wait_ge(s_w, 6 * DC)
            for u in range(U):
                if u == 1:
                    pe.wait_ge(s_drow, 2)
                if u >= NZ:
                    pe.wait_ge(s_z, u - NZ + 1)
                project(u, u)
            with pe.Fori(1, NG) as i:
                for u in range(U):
                    pe.wait_ge(s_z, i * U + u - NZ + 1)
                    project(u, i * U + u)

            pe.wait_ge(s_chosen, NG)
            chosen_all = chosen[:].rearrange("p e n -> p (e n)")
            pe.matmul(rank_ps[:, 0:NT * E], before[:], chosen_all, start=True, stop=True).then_inc(s_rank, 1)
            pe.matmul(total_ps[:, 0:NT * E], ones_bf[:], chosen_all, start=True, stop=True).then_inc(s_rank, 1)
            pe.wait_ge(s_colof, 4)
            for g in range(NTG):
                ins = pe.matmul(col_ps[:, g:g + 1],
                                col_of[:, g * TG:(g + 1) * TG].rearrange("p t s e o -> p (t s e o)"),
                                ident_bf[:, 0:1], start=True, stop=True)
            ins.then_inc(s_colps, 1)

            def table_of(i):
                pe.wait_ge(s_psb, i + 1)
                for g in range(i * BG, (i + 1) * BG):
                    if g < POOL_COLS:
                        pe.wait_ge(s_colhot, g + 1)
                    else:
                        pe.wait_ge(s_colhot2, g + 1 - POOL_COLS)
                    ins = pe.matmul(table_ps[:, 0:NSC], partial[:, g * P:(g + 1) * P], col_hot[:, g, :],
                                    start=(g == 0), stop=(g == NTG - 1))
                if i == NTG // BG - 1:
                    ins.then_inc(s_tab, 1)

            pe.wait_ge(s_hot2, TOPK)
            for g in range(NTG):
                if g in ACT_GROUPS:
                    n = ACT_GROUPS.index(g)
                    pe.wait_ge(s_rowhot2, n + 1)
                    rows = row_hot2[n % AHOT]
                else:
                    n = DVE_GROUPS.index(g)
                    pe.wait_ge(s_rowhot, n + 1)
                    rows = row_hot[n % HOT]
                for t in range(TG):
                    for k in range(TOPK):
                        ins = pe.matmul(part_ps[g // BG][t * JW:(t + 1) * JW, (g % BG) * P:(g % BG + 1) * P],
                                        hot[:, k, g * TG + t].rearrange("p s e o -> p (s e o)"),
                                        rows[:, t, k, :], start=(k == 0), stop=(k == TOPK - 1))
                ins.then_inc(s_part, 1)
                if g % BG == 2 and g > BG:
                    table_of(g // BG - 1)
            table_of(NTG // BG - 1)

            n = blocks_of(pe)

            def transpose_z(b):
                pe.wait_ge(s_get, (b + 1) * (16 * Q))
                for c in range(DC):
                    for q in range(Q):
                        ins = pe.transpose(zt_ps[c][:, q * P:(q + 1) * P], z_row[:, q, c * P:(c + 1) * P], ident[:])
                ins.then_inc(s_zt, 1)

            def w1(part, c, dc):
                o = dc * CQ * P + (c % CQ) * P
                return part[c // CQ][:, o:o + P]

            def w2(part, c):
                o = W1Q + (c % CQ) * D
                return part[c // CQ][:, o:o + D]

            def first_product(b, c, fresh):
                if c % CQ == 0:
                    pe.wait_ge(s_wlo, (b + 1) * NQ + c // CQ + 1)
                if not (fresh and c < NHP):
                    pe.wait_ge(s_relu, b * HC + c + 1 - back(c))
                hp = h_ps[c % NHP][:, 0:TB]
                for dc in range(DC):
                    if c == 0:
                        pe.wait_ge(s_zlo, b * DC + dc + 1)
                    pe.matmul(hp, w1(w_hi, c, dc), z_hi[:, dc, :], start=(dc == 0), stop=False)
                    pe.matmul(hp, w1(w_hi, c, dc), z_lo[:, dc, :], start=False, stop=False)
                    ins = pe.matmul(hp, w1(w_lo, c, dc), z_hi[:, dc, :], start=False, stop=(dc == DC - 1))
                ins.then_inc(s_h1, 1)

            def second_product(b, c, fresh):
                pe.wait_ge(s_hlo, b * HC + c + 1)
                if c == 0 and not fresh:
                    pe.wait_ge(s_y, b * Q)
                for q in range(Q):
                    hi = h_hi[c % NHX][:, q * P:(q + 1) * P]
                    lo = h_lo[c % NHX][:, q * P:(q + 1) * P]
                    yp = y_ps[q][:, 0:D]
                    pe.matmul(yp, hi, w2(w_hi, c), start=(c == 0), stop=False)
                    pe.matmul(yp, hi, w2(w_lo, c), start=False, stop=False)
                    ins = pe.matmul(yp, lo, w2(w_hi, c), start=False, stop=(c == HC - 1))
                ins.then_inc(s_h2, 1)

            def block_of_pe(b, fresh):
                for c in range(HC):
                    if c == (HC - 1 if fresh else 2):
                        transpose_z(b + 1)
                    first_product(b, c, fresh)
                    if c >= LAG:
                        second_product(b, c - LAG, fresh)
                for c in range(HC - LAG, HC):
                    second_product(b, c, fresh)

            transpose_z(0)
            block_of_pe(0, True)
            with pe.Fori(1, n) as b:
                block_of_pe(b, False)


def kernel(**inputs):
    import numpy as _np
    import concourse.bacc as _bacc
    from concourse import mybir as _mybir
    from concourse.bass_utils import run_bass_kernel_spmd as _run

    P = 128
    Q = 3
    a = {k: _np.asarray(v) for k, v in inputs.items()}
    x = a["x"]
    B, S, D = x.shape
    w = a["L0_cond_weight"]
    W1, W2 = a["L0_ffn_W1"], a["L0_ffn_W2"]
    E, _, H = W1.shape
    HC, DC, NQ = H // P, D // P, 4
    q1 = W1.reshape(E, DC, P, NQ, H // NQ).transpose(0, 3, 2, 1, 4).reshape(E, NQ, P, -1)
    q2 = W2.reshape(E, NQ, HC // NQ, P, D).transpose(0, 1, 3, 2, 4).reshape(E, NQ, P, -1)
    arrays = {
        "x": x.reshape(B * S, D),
        "xT": x.reshape(B * S, DC, P).transpose(2, 1, 0),
        "condT": a["cond_1024"].reshape(B, DC, P).transpose(2, 1, 0),
        "w": w,
        "wT": w.T,
        "wr": a["L0_ffn_Wr"],
        "br": a["L0_ffn_br"],
        "experts": _np.concatenate([q1, q2], axis=3),
        "b1": a["L0_ffn_b1"].reshape(E, HC, P).transpose(2, 0, 1),
        "b2": a["L0_ffn_b2"],
    }
    NT = B * S // P
    JW = 4 * E
    j, g = _np.arange(P)[:, None], _np.arange(NT * JW // P)[None, :]
    tile = g * (P // JW) + j // JW
    arrays["slot_weight"] = _np.where(j // (2 * E) % 2 == 0, P * tile, 1).astype(_np.float32)
    arrays = {f"in_{k}": _np.ascontiguousarray(v) for k, v in arrays.items()}
    nc = _bacc.Bacc("TRN2", target_bir_lowering=False, num_devices=1)
    args = [nc.dram_tensor(k, v.shape, _mybir.dt.from_np(v.dtype), kind="ExternalInput").ap()
            for k, v in arrays.items()]
    out = nc.dram_tensor("out", (B * S + Q * P, D), _mybir.dt.from_np(x.dtype), kind="ExternalOutput").ap()
    bass_adaln_moe_ffn(nc, *args, out)
    r = _run(nc, [arrays], core_ids=[0])
    return r.results[0]["out"][:B * S].reshape(B, S, D)
```
